# Optimizing a Trainium2 kernel written in Bass

```python
import numpy as np
import jax
import jax.numpy as jnp

def _softmax(x, axis=-1):
    return jax.nn.softmax(x, axis=axis)

def _gelu(x):
    return jax.nn.gelu(x, approximate=True)

def _silu(x):
    return jax.nn.silu(x)

def _sigmoid(x):
    return jax.nn.sigmoid(x)

def _layernorm(x, axis=-1, eps=1e-05):
    m = jnp.mean(x, axis=axis, keepdims=True)
    v = jnp.var(x, axis=axis, keepdims=True)
    return (x - m) / jnp.sqrt(v + eps)

def _scatter_add(tgt, idx, src, axis=0):
    return tgt.at[idx].add(src)

def _segment_sum(src, seg, n):
    return jax.ops.segment_sum(src, seg, n)
kernel_name = 'mk_adaln_d1_jaxref_r8_1d2f2d'

def setup_inputs(seed: int=0):
    np.random.seed(seed)
    _w = jnp.asarray

    def _L0_attn_setup():
        import jax, jax.numpy as jnp
        import numpy as np
        DIM = 128
        HEADS = 16
        DIM_HEAD = 64
        DIM_INNER = HEADS * DIM_HEAD
        SCALE = DIM_HEAD ** (-0.5)

        def rmsnorm(x, w):
            eps = jnp.asarray(jnp.finfo(x.dtype).eps, x.dtype)
            var = jnp.mean(jnp.square(x), axis=-1, keepdims=True)
            return x * jax.lax.rsqrt(var + eps) * w
        key = jax.random.key(seed)
        ks = jax.random.split(key, 6)
        tokens = jax.random.normal(ks[0], (2, 256, DIM), dtype=jnp.float32)
        norm_w = jnp.ones((DIM,), dtype=jnp.float32)
        Wq = jax.random.normal(ks[1], (DIM, DIM_INNER), dtype=jnp.float32) * 0.02
        Wkv = jax.random.normal(ks[2], (DIM, 2 * DIM_INNER), dtype=jnp.float32) * 0.02
        Wout = jax.random.normal(ks[3], (DIM_INNER, DIM), dtype=jnp.float32) * 0.02
        Wg = jax.random.normal(ks[4], (DIM, HEADS), dtype=jnp.float32) * 0.02
        return {'tokens': tokens, 'norm_w': norm_w, 'Wq': Wq, 'Wkv': Wkv, 'Wout': Wout, 'Wg': Wg}
    _L0_attn_in = _L0_attn_setup()

    def _L0_ffn_setup():
        import jax, jax.numpy as jnp
        import numpy as np
        B, T, D = (2, 256, 128)
        DCD = 512
        RET = 128
        NEXP = 512
        NKEYS = 64
        H = 4
        KPH = 8
        key = jax.random.key(seed)
        ks = jax.random.split(key, 10)
        s = lambda k, shape, scale: jax.random.normal(k, shape, jnp.float32) * scale
        return {'hidden_states': jax.random.normal(ks[0], (B, T, D), jnp.float32), 'Wg': s(ks[1], (D, DCD), 0.02), 'bg': jnp.zeros((DCD,), jnp.float32), 'Wu': s(ks[2], (D, DCD), 0.02), 'bu': jnp.zeros((DCD,), jnp.float32), 'Wd': s(ks[3], (DCD, D), 0.02), 'bd': jnp.zeros((D,), jnp.float32), 'Wq': s(ks[4], (D, RET * H), 0.02), 'keys': s(ks[5], (H, NKEYS, 2, RET // 2), 0.02), 'down_embed': s(ks[6], (NEXP, D), 0.02), 'up_embed': s(ks[7], (NEXP, D), 0.02)}
    _L0_ffn_in = _L0_ffn_setup()
    _L0_c = _w((lambda *s: np.random.randn(*s).astype(np.float32) * 0.05)(32, 128))
    _L0_wmod = _w((lambda *s: np.random.randn(*s).astype(np.float32) * 0.05)(128, 6 * 128) * 128 ** (-0.5))
    _d = {'L0_attn_tokens': _L0_attn_in['tokens'], 'L0_attn_norm_w': _L0_attn_in['norm_w'], 'L0_attn_Wq': _L0_attn_in['Wq'], 'L0_attn_Wkv': _L0_attn_in['Wkv'], 'L0_attn_Wout': _L0_attn_in['Wout'], 'L0_attn_Wg': _L0_attn_in['Wg'], 'L0_ffn_Wg': _L0_ffn_in['Wg'], 'L0_ffn_bg': _L0_ffn_in['bg'], 'L0_ffn_Wu': _L0_ffn_in['Wu'], 'L0_ffn_bu': _L0_ffn_in['bu'], 'L0_ffn_Wd': _L0_ffn_in['Wd'], 'L0_ffn_bd': _L0_ffn_in['bd'], 'L0_ffn_Wq': _L0_ffn_in['Wq'], 'L0_ffn_keys': _L0_ffn_in['keys'], 'L0_ffn_down_embed': _L0_ffn_in['down_embed'], 'L0_ffn_up_embed': _L0_ffn_in['up_embed'], 'L0_c': _L0_c, 'L0_wmod': _L0_wmod}
    _x0 = _d['L0_attn_tokens']
    _d['L0_attn_tokens'] = jax.random.normal(jax.random.fold_in(jax.random.key(seed), 1), (32, 256, 128), dtype=_x0.dtype)
    del _x0
    return _d

def reference(L0_attn_tokens, L0_attn_norm_w, L0_attn_Wq, L0_attn_Wkv, L0_attn_Wout, L0_attn_Wg, L0_ffn_Wg, L0_ffn_bg, L0_ffn_Wu, L0_ffn_bu, L0_ffn_Wd, L0_ffn_bd, L0_ffn_Wq, L0_ffn_keys, L0_ffn_down_embed, L0_ffn_up_embed, L0_c, L0_wmod):

    def _L0_attn_ref(tokens, norm_w, Wq, Wkv, Wout, Wg):
        import jax, jax.numpy as jnp
        import numpy as np
        DIM = 128
        HEADS = 16
        DIM_HEAD = 64
        DIM_INNER = HEADS * DIM_HEAD
        SCALE = DIM_HEAD ** (-0.5)

        def rmsnorm(x, w):
            eps = jnp.asarray(jnp.finfo(x.dtype).eps, x.dtype)
            var = jnp.mean(jnp.square(x), axis=-1, keepdims=True)
            return x * jax.lax.rsqrt(var + eps) * w
        b, n, _ = tokens.shape
        x = rmsnorm(tokens, norm_w)
        q = x @ Wq
        kv = x @ Wkv
        k, v = jnp.split(kv, 2, axis=-1)

        def split_heads(t):
            return t.reshape(b, n, HEADS, DIM_HEAD).transpose(0, 2, 1, 3)
        q, k, v = map(split_heads, (q, k, v))
        sim = jnp.einsum('bhid,bhjd->bhij', q, k) * SCALE
        causal_mask = jnp.triu(jnp.ones((n, n), dtype=bool), k=1)
        sim = jnp.where(causal_mask, jnp.asarray(-jnp.finfo(sim.dtype).max, sim.dtype), sim)
        attn = jax.nn.softmax(sim, axis=-1)
        out = jnp.einsum('bhij,bhjd->bhid', attn, v)
        gates = jax.nn.sigmoid(x @ Wg)
        gates = gates.transpose(0, 2, 1)[..., None]
        out = gates * out
        out = out.transpose(0, 2, 1, 3).reshape(b, n, DIM_INNER)
        return out @ Wout

    def _L0_ffn_ref(hidden_states, Wg, bg, Wu, bu, Wd, bd, Wq, keys, down_embed, up_embed):
        import jax, jax.numpy as jnp
        import numpy as np
        B, T, D = (2, 256, 128)
        DCD = 512
        RET = 128
        NEXP = 512
        NKEYS = 64
        H = 4
        KPH = 8
        b, t, d = hidden_states.shape
        q = (hidden_states @ Wq).reshape(b, t, 2, H, RET // 2)
        sim = jnp.einsum('btphn,hkpn->pbthk', q, keys)
        sc, ix = jax.lax.top_k(sim, KPH)
        sx, sy = (sc[0], sc[1])
        ixx, ixy = (ix[0], ix[1])
        all_sc = (sx[..., :, None] + sy[..., None, :]).reshape(b, t, H, KPH * KPH)
        all_ix = (ixx[..., :, None] * NKEYS + ixy[..., None, :]).reshape(b, t, H, KPH * KPH)
        scores, pk = jax.lax.top_k(all_sc, KPH)
        idx = jnp.take_along_axis(all_ix, pk, axis=-1)
        de = down_embed[idx]
        ue = up_embed[idx]
        w = jnp.einsum('btd,bthkd->bthk', hidden_states, de)
        w = jax.nn.silu(w) * jax.nn.softmax(scores, axis=-1)
        experts_states = jnp.einsum('bthk,bthkd->btd', w, ue)
        mlp = jax.nn.silu(hidden_states @ Wg + bg) * (hidden_states @ Wu + bu) @ Wd + bd
        return mlp + experts_states
    x = L0_attn_tokens
    mod = (_silu(L0_c) @ L0_wmod).reshape(L0_c.shape[0], 6, 1, -1)
    sa, ca, ga, sb, cb, gb = (mod[:, 0], mod[:, 1], mod[:, 2], mod[:, 3], mod[:, 4], mod[:, 5])
    ga = (2 * (ga >= 0) - 1) * jnp.maximum(jnp.abs(ga), 0.25)
    gb = (2 * (gb >= 0) - 1) * jnp.maximum(jnp.abs(gb), 0.25)
    h = _layernorm(x, axis=-1) * (1 + ca) + sa
    x = x + ga * _L0_attn_ref(h, L0_attn_norm_w, L0_attn_Wq, L0_attn_Wkv, L0_attn_Wout, L0_attn_Wg)
    h = _layernorm(x, axis=-1) * (1 + cb) + sb
    x = x + gb * _L0_ffn_ref(h, L0_ffn_Wg, L0_ffn_bg, L0_ffn_Wu, L0_ffn_bu, L0_ffn_Wd, L0_ffn_bd, L0_ffn_Wq, L0_ffn_keys, L0_ffn_down_embed, L0_ffn_up_embed)
    return x

_drawn_inputs = setup_inputs


def setup_inputs(seed=0):
    import zlib

    import numpy as np

    out = dict(_drawn_inputs(seed))
    spreads = {'L0_attn_norm_w': (1.0, 0.6),
     'L0_ffn_bg': (0.0, 0.8),
     'L0_ffn_bu': (0.0, 0.8),
     'L0_ffn_bd': (0.0, 0.998)}
    factors = {'L0_attn_Wq': 8.0,
     'L0_attn_Wkv': 8.0,
     'L0_attn_Wout': 8.0,
     'L0_attn_Wg': 8.0,
     'L0_ffn_Wg': 8.0,
     'L0_ffn_Wu': 8.0,
     'L0_ffn_Wd': 8.0,
     'L0_ffn_Wq': 56.703,
     'L0_ffn_keys': 54.911,
     'L0_ffn_down_embed': 8.0,
     'L0_ffn_up_embed': 8.0}
    for name, (base, spread) in spreads.items():
        noise = np.random.default_rng([zlib.crc32(name.encode()), seed]).standard_normal(out[name].shape)
        drawn = base * np.exp(spread * noise) if base else spread * noise
        out[name] = jnp.asarray(drawn.astype(out[name].dtype))
    for name, factor in factors.items():
        out[name] = (out[name] * factor).astype(out[name].dtype)
    return out
```

```python
import concourse.bass as bass
from concourse import mybir
from contextlib import ExitStack

F32 = mybir.dt.float32
BF16 = mybir.dt.bfloat16
ALU = mybir.AluOpType
ACT = mybir.ActivationFunctionType
AX_X = mybir.AxisListType.X

B, N, D = 32, 256, 128
P = 128
TB = N // P
H, DH = 16, 64
NP = H // 2
DI = H * DH
BLOCKS = TB * (TB + 1) // 2
SW = BLOCKS * P
F = 512
FC = F // P
NE = 512
EC = NE // P
RH, NK, KD, TK = 4, 64, 64, 8
NX = NE // NK
SCALE = float(DH) ** -0.5
LN_EPS = 1e-5
RMS_EPS = 2.0 ** -23
MASKED = -1e30
NSTEP = NP + 3
BANK = 512
NMOD = 7
SA, CA, SB, CB, GA, GB, GD = range(NMOD)


def program(nc, x, norm_w, Wq, Wkv, Wout, Wgate, fWg, fbg, fWu, fbu, fWd, fbd, fWq, keys,
            down, up, cond, wmod, out):
    ctx = ExitStack()
    with ctx:
        def sb(name, shape, dt=F32):
            return ctx.enter_context(nc.sbuf_tensor(name, shape, dt))

        def sem(name):
            return ctx.enter_context(nc.semaphore(name))

        ident = sb("ident", [P, P])
        ident_bf = sb("ident_bf", [P, P], BF16)
        mask = sb("mask", [P, P], BF16)
        expo = sb("expo", [P, TB])
        w_qkv = sb("w_qkv", [P, 3 * DI])
        w_gate = sb("w_gate", [P, H])
        nw = sb("nw", [P, 1])
        w_out = sb("w_out", [P, NP, D])
        w_g = sb("w_g", [P, F])
        w_u = sb("w_u", [P, F])
        b_g = sb("b_g", [P, FC])
        b_gh = sb("b_gh", [P, FC])
        b_u = sb("b_u", [P, FC])
        w_d = sb("w_d", [P, FC, D])
        w_up = sb("w_up", [P, EC, D])
        w_down = sb("w_down", [P, NE])
        w_sim = sb("w_sim", [P, 2 * RH * NK])

        fwq_sb = sb("fwq_sb", [P, RH, 2, KD])
        fwqT = sb("fwqT", [P, RH * D])
        key_sb = sb("key_sb", [NK, RH, 2 * KD])
        keyT = sb("keyT", [P, RH * NK])
        down_sb = sb("down_sb", [P, EC, D])
        c_sb = sb("c_sb", [B, D])
        c_th = sb("c_th", [B, D])
        c_silu = sb("c_silu", [B, D])
        cT = sb("cT", [P, B])
        wmod_sb = sb("wmod_sb", [P, 6 * D])
        mod_sb = sb("mod_sb", [B, 6 * D])
        mods = sb("mods", [B, NMOD, D])
        sgn = sb("sgn", [B, 2, D])
        mag = sb("mag", [B, 2, D])
        bd_sb = sb("bd_sb", [B, D])
        mods_dram = nc.dram_tensor("mods_dram", [B, NMOD * D], F32, kind="Internal").ap()

        x_in = sb("x_in", [P, TB, D])
        x_res = sb("x_res", [P, TB, D])
        modA = sb("modA", [P, 2, D])
        modB = sb("modB", [P, 3, D])
        modC = sb("modC", [P, 2, D])
        st1 = sb("st1", [P, TB, 6])
        mv1 = sb("mv1", [P, TB, 2])
        ve1 = sb("ve1", [P, TB])
        rs1 = sb("rs1", [P, TB])
        h1 = sb("h1", [P, TB, D])
        sq1 = sb("sq1", [P, TB, D])
        ms1 = sb("ms1", [P, TB])
        me1 = sb("me1", [P, TB])
        rr1 = sb("rr1", [P, TB])
        xr = sb("xr", [P, TB, D])
        xT = sb("xT", [P, N])
        qk = sb("qk", [P, 4, 2 * N])
        v = sb("v", [P, TB, H, DH + 1])
        s_sb = sb("s_sb", [P, 2, 2, SW])
        mx = sb("mx", [P, 2, 2, TB])
        pT = sb("pT", [P, 2, 2, SW])
        g_th = sb("g_th", [P, TB, H])
        rden = sb("rden", [P, 2, TB])
        coef = sb("coef", [P, 2, TB])
        ao = sb("ao", [P, 2, TB, P])
        aoT = sb("aoT", [P, NP, N])
        ga_o = sb("ga_o", [P, TB, D])
        x2 = sb("x2", [P, TB, D])
        x2g = sb("x2g", [P, TB, D])
        st2 = sb("st2", [P, TB, 6])
        mv2 = sb("mv2", [P, TB, 2])
        ve2 = sb("ve2", [P, TB])
        rs2 = sb("rs2", [P, TB])
        h2 = sb("h2", [P, TB, D])
        h2T = sb("h2T", [P, N])
        sim = sb("sim", [P, TB, 2, RH, NK])
        tops = sb("tops", [P, 2, TB, RH, TK])
        big = sb("big", [P, TB, RH, 1])
        sx = sb("sx", [P, TB, RH, TK])
        xs = sb("xs", [P, TB, RH, NX])
        cand = sb("cand", [P, TB, RH, TK, TK])
        top8 = sb("top8", [P, TB, RH, TK])
        e8 = sb("e8", [P, TB, RH, TK])
        zz = sb("zz", [P, TB, RH])
        rz = sb("rz", [P, TB, RH])
        fsum = sb("fsum", [P, TB, RH, NX, NK])
        fexp = sb("fexp", [P, TB, RH, NE])
        wsum = sb("wsum", [P, TB, NE])
        tot = sb("tot", [P, TB])
        u_sb = sb("u_sb", [P, FC, N])
        g_t = sb("g_t", [P, FC, N])
        gu = sb("gu", [P, FC, N])
        m_sb = sb("m_sb", [P, FC, N])
        d_t = sb("d_t", [P, TB, NE])
        d_s = sb("d_s", [P, TB, NE])
        eo = sb("eo", [P, TB, NE])
        eT = sb("eT", [P, TB, EC, P])
        y_g = sb("y_g", [P, TB, D])
        yo = sb("yo", [P, TB, D])

        pS = [ctx.enter_context(nc.psum_tensor(f"pS{n}", [P, 2, BANK], F32)) for n in range(2)]
        pTT = ctx.enter_context(nc.psum_tensor("pTT", [P, 2, BANK], F32))
        pW = [ctx.enter_context(nc.psum_tensor(f"pW{n}", [P, BANK], F32)) for n in range(2)]

        load_qkv, load_w, load_c = sem("load_qkv"), sem("load_w"), sem("load_c")
        const_pool, const_dve = sem("const_pool"), sem("const_dve")
        su_pe, su_act, su_dve = sem("su_pe"), sem("su_act"), sem("su_dve")
        mods_stored = sem("mods_stored")

        per = {}

        def ev(name, n):
            s = sem(name)
            per[name] = (s, n)
            return name

        def at(name, batch, k):
            return batch * per[name][1] + k

        def S(name):
            return per[name][0]

        x_loaded, res_loaded = ev("x_loaded", 16), ev("res_loaded", 16)
        modA_loaded, modB_loaded, modC_loaded = ev("modA_loaded", 16), ev("modB_loaded", 16), ev("modC_loaded", 16)
        out_stored = ev("out_stored", 16)
        ln1_chain, attn_chain, ffn_chain = ev("ln1_chain", LN1_LINKS), ev("attn_chain", ATTN_LINKS), ev("ffn_chain", FFN_LINKS)
        rstd1_in, rstd1_out = ev("rstd1_in", 2), ev("rstd1_out", 2)
        pool_chain1, pool_chain2 = ev("pool_chain1", 2), ev("pool_chain2", 1)
        xr_ready = ev("xr_ready", 1)
        s_full, s_taken = ev("s_full", NP), ev("s_taken", NP)
        t_full, exp_done = ev("t_full", NP), ev("exp_done", NP)
        gate_done = ev("gate_done", 1)
        ao_ready = ev("ao_ready", NP)
        x2_ready, x2g_ready = ev("x2_ready", 1), ev("x2g_ready", 1)
        rstd2_in, rstd2_out = ev("rstd2_in", 1), ev("rstd2_out", 1)
        h2_ready = ev("h2_ready", 1)
        top_ready, xs_ready = ev("top_ready", 1), ev("xs_ready", 1)
        f_ready, fexp_ready, e8_ready = ev("f_ready", TB), ev("fexp_ready", TB), ev("e8_ready", 1)
        wsum_ready = ev("wsum_ready", TB)
        gu_act, gu_ready = ev("gu_act", FC), ev("gu_ready", 1)
        d_act = ev("d_act", TB)
        eo_ready = ev("eo_ready", TB)
        yo_ready = ev("yo_ready", 1)

        def jobs_of(step):
            js = []
            if step < 0:
                js += [("xT", 0, "a"), ("op", 0, "f"), ("QK", 0, "a"), ("QK", 1, "a")]
                js += [("V", n, "a") for n in range(2 * TB)]
                return js
            if step + 2 < NP:
                js.append(("QK", step + 2, "a"))
            ffn = {1: [("hT", 0)], 2: [("sim", 0), ("sim", 1)], 3: [("GU", 0)], 4: [("GU", 1)], 5: [("GU", 2)],
                   6: [("GU", 3)], 7: [("D", 0)], 8: [("D", 1)], 9: [("ET", 0)], 10: [("ET", 1)]}
            js += [(n, k, "f") for n, k in ffn.get(step, [])]
            if 2 <= step < NP + 2:
                js.append(("PV", step - 2, "a"))
            if 3 <= step < NP + 3:
                js.append(("AO", step - 3, "a"))
            if step == NSTEP - 1:
                js.append(("y", 0, "f"))
            return js

        order = [j for step in range(-1, NSTEP) for j in jobs_of(step)]
        assert len(order) % 2 == 0
        bank_of, place, count = {}, {}, {}
        for n, (name, k, kind) in enumerate(order):
            key = (n % 2, kind)
            bank_of[name, k] = n % 2
            place[name, k] = count.get(key, 0)
            count[key] = place[name, k] + 1
        work_full = {key: ev(f"work_full_{key[1]}{key[0]}", n) for key, n in count.items()}
        work_free = {key: ev(f"work_free_{key[1]}{key[0]}", n) for key, n in count.items()}
        kind_of = {(name, k): kind for name, k, kind in order}

        class Work:

            def __init__(self, eng, i, attn, ffn):
                self.eng, self.i, self.attn, self.ffn = eng, i, attn, ffn

            def key(self, name, k):
                return bank_of[name, k], kind_of[name, k]

            def batch(self, name, k):
                return self.i if kind_of[name, k] == "a" else self.i - 1

            def bank(self, name, k=0):
                return pW[bank_of[name, k]]

            def before(self, name, k):
                mine = [j for j in order if bank_of[j[0], j[1]] == bank_of[name, k]]
                now = [j for j in mine if (self.attn if j[2] == "a" else self.ffn)]
                n = [(j[0], j[1]) for j in now].index((name, k))
                if n:
                    return now[n - 1][:2], self.batch(*now[n - 1][:2])
                if not self.ffn:
                    return None
                j = [j for j in mine if not self.first_loop or j[2] == "a"][-1]
                return j[:2], (self.i if j[2] == "a" else self.i - 1) - 1

            first_loop = False

            def wait_free(self, name, k=0):
                prev = self.before(name, k)
                if prev:
                    (pn, pk), batch = prev
                    ev_ = work_free[self.key(pn, pk)]
                    self.eng.wait_ge(S(ev_), at(ev_, batch, place[pn, pk] + 1))

            def filled(self, ins, name, k=0):
                ins.then_inc(S(work_full[self.key(name, k)]), 1)

            def wait_full(self, name, k=0):
                e = work_full[self.key(name, k)]
                self.eng.wait_ge(S(e), at(e, self.batch(name, k), place[name, k] + 1))

            def release(self, ins, name, k=0):
                ins.then_inc(S(work_free[self.key(name, k)]), 1)

        def run(eng, body):
            body(0, True, False, False)
            body(1, True, True, True)
            with eng.Fori(2, B - 1) as i:
                body(i, True, True, False)
            body(B - 1, True, True, False)
            body(B, False, True, False)

        block = ctx.enter_context(nc.Block())

        @block.sync
        def _(sp):
            sp.dma_start(w_qkv[:, 0:DI], Wq).then_inc(load_qkv, 16)
            sp.dma_start(w_qkv[:, DI:3 * DI], Wkv).then_inc(load_qkv, 16)
            sp.dma_start(w_gate[:, :], Wgate).then_inc(load_qkv, 16)
            sp.dma_start(nw[:, :], norm_w.rearrange("(d o) -> d o", o=1), allow_slow_non_contiguous=True).then_inc(load_qkv, 16)
            sp.dma_start(w_out[:, :, :], Wout.rearrange("(j p) n -> p j n", p=P)).then_inc(load_w, 16)
            sp.dma_start(w_g[:, :], fWg).then_inc(load_w, 16)
            sp.dma_start(w_u[:, :], fWu).then_inc(load_w, 16)
            sp.dma_start(b_g[:, :], fbg.rearrange("(c p) -> p c", p=P), allow_slow_non_contiguous=True).then_inc(load_w, 16)
            sp.dma_start(b_u[:, :], fbu.rearrange("(c p) -> p c", p=P), allow_slow_non_contiguous=True).then_inc(load_w, 16)
            sp.dma_start(w_d[:, :, :], fWd.rearrange("(c p) n -> p c n", p=P)).then_inc(load_w, 16)
            sp.dma_start(w_up[:, :, :], up.rearrange("(c p) n -> p c n", p=P)).then_inc(load_w, 16)

            def load_next(b):
                sp.dma_start(x_in[:, :, :], x[bass.ds(b, 1)].rearrange("o (k p) d -> p (o k) d", p=P)).then_inc(S(x_loaded), 16)
                sp.dma_start(modA[:, :, :].rearrange("p m d -> p (m d)"),
                             mods_dram[bass.ds(b, 1), SA * D:(CA + 1) * D].broadcast_to([P, 2 * D])).then_inc(S(modA_loaded), 16)

            sp.wait_ge(su_dve, SU_LINKS)
            sp.dma_start(mods_dram, mods[:, :, :].rearrange("b m d -> b (m d)")).then_inc(mods_stored, 16)
            sp.wait_ge(mods_stored, 16)
            load_next(0)

            def body(i, attn, ffn, first):
                if attn:
                    if ffn:
                        sp.wait_ge(S(x2_ready), at(x2_ready, i - 1, 1))
                        sp.wait_ge(S(h2_ready), at(h2_ready, i - 1, 1))
                    sp.dma_start(x_res[:, :, :], x[bass.ds(i, 1)].rearrange("o (k p) d -> p (o k) d", p=P)).then_inc(S(res_loaded), 16)
                    sp.dma_start(modB[:, :, :].rearrange("p m d -> p (m d)"),
                                 mods_dram[bass.ds(i, 1), SB * D:(GA + 1) * D].broadcast_to([P, 3 * D])).then_inc(S(modB_loaded), 16)
                    if not (isinstance(i, int) and i + 1 >= B):
                        sp.wait_ge(S(xr_ready), at(xr_ready, i, 1))
                        load_next(i + 1)
                if ffn:
                    sp.wait_ge(S(yo_ready), at(yo_ready, i - 1, 1))
                    sp.dma_start(out[bass.ds(i - 1, 1)].rearrange("o (k p) d -> p (o k) d", p=P), yo[:, :, :]).then_inc(S(out_stored), 16)
                if attn:
                    sp.dma_start(modC[:, :, :].rearrange("p m d -> p (m d)"),
                                 mods_dram[bass.ds(i, 1), GB * D:(GD + 1) * D].broadcast_to([P, 2 * D])).then_inc(S(modC_loaded), 16)

            run(sp, body)
            sp.wait_ge(S(out_stored), at(out_stored, B, 0))

        @block.gpsimd
        def _(pool):
            nc.gpsimd.memset(ident[:, :], 0.0)
            nc.gpsimd.memset(ident_bf[:, :], 0.0)
            nc.gpsimd.memset(mask[:, :], 0.0)
            nc.gpsimd.memset(expo[:, :], -0.5)
            nc.gpsimd.memset(v[:, :, :, DH:DH + 1], 1.0).then_inc(const_pool, 1)
            pool.wait_ge(const_pool, 1)
            nc.gpsimd.affine_select(out=ident[:, :], in_=ident[:, :], compare_op=ALU.not_equal, fill=1.0,
                                    base=0, pattern=[[-1, P]], channel_multiplier=1)
            nc.gpsimd.affine_select(out=ident_bf[:, :], in_=ident_bf[:, :], compare_op=ALU.not_equal, fill=1.0,
                                    base=0, pattern=[[-1, P]], channel_multiplier=1)
            nc.gpsimd.affine_select(out=mask[:, :], in_=mask[:, :], compare_op=ALU.is_ge, fill=MASKED,
                                    base=0, pattern=[[-1, P]], channel_multiplier=1).then_inc(const_pool, 1)

            def apart():
                pool.nop(nofuse=True)

            def rstd1(b):
                pool.wait_ge(S(rstd1_in), at(rstd1_in, b, 1))
                apart()
                nc.gpsimd.tensor_scalar(ve1[:, :], mv1[:, :, 1], LN_EPS, None, ALU.add).then_inc(S(pool_chain1), 1)
                pool.wait_ge(S(pool_chain1), at(pool_chain1, b, 1))
                nc.gpsimd.tensor_tensor(rs1[:, :], ve1[:, :], expo[:, :], ALU.pow).then_inc(S(rstd1_out), 1)
                pool.wait_ge(S(rstd1_in), at(rstd1_in, b, 2))
                apart()
                nc.gpsimd.tensor_scalar(me1[:, :], ms1[:, :], 1.0 / D, RMS_EPS, ALU.mult, ALU.add).then_inc(S(pool_chain1), 1)
                pool.wait_ge(S(pool_chain1), at(pool_chain1, b, 2))
                nc.gpsimd.tensor_tensor(rr1[:, :], me1[:, :], expo[:, :], ALU.pow).then_inc(S(rstd1_out), 1)

            rstd1(0)

            def body(i, attn, ffn, first):
                f = i - 1
                if ffn:
                    pool.wait_ge(S(rstd2_in), at(rstd2_in, f, 1))
                    apart()
                    nc.gpsimd.tensor_scalar(ve2[:, :], mv2[:, :, 1], LN_EPS, None, ALU.add).then_inc(S(pool_chain2), 1)
                    pool.wait_ge(S(pool_chain2), at(pool_chain2, f, 1))
                    nc.gpsimd.tensor_tensor(rs2[:, :], ve2[:, :], expo[:, :], ALU.pow).then_inc(S(rstd2_out), 1)
                    pool.wait_ge(S(x2_ready), at(x2_ready, f, 1))
                    pool.wait_ge(S(modC_loaded), at(modC_loaded, f, 16))
                    nc.gpsimd.tensor_tensor(x2g[:, :, :], x2[:, :, :], modC[:, 1:2, :].broadcast_to([P, TB, D]),
                                            ALU.add).then_inc(S(x2g_ready), 1)
                if attn and not (isinstance(i, int) and i + 1 >= B):
                    rstd1(i + 1)
                if ffn:
                    pool.wait_ge(S(xs_ready), at(xs_ready, f, 1))
                    for k in range(TB):
                        for h in range(RH):
                            ins = nc.gpsimd.tensor_tensor(
                                fsum[:, k, h], xs[:, k, h, :].unsqueeze(2).broadcast_to([P, NX, NK]),
                                sim[:, k, 1, h, :].unsqueeze(1).broadcast_to([P, NX, NK]), ALU.add)
                        ins.then_inc(S(f_ready), 1)
                    for k in range(TB):
                        pool.wait_ge(S(wsum_ready), at(wsum_ready, f, k + 1))
                        e = work_free[bank_of["D", k], "f"]
                        pool.wait_ge(S(e), at(e, f, place["D", k] + 1))
                        nc.gpsimd.tensor_tensor(eo[:, k, :], d_s[:, k, :], wsum[:, k, :], ALU.mult).then_inc(S(eo_ready), 1)

            run(pool, body)

        @block.scalar
        def _(act):
            act.dma_start(c_sb[:, :], cond).then_inc(load_c, 16)
            act.dma_start(wmod_sb[:, :], wmod).then_inc(load_c, 16)
            act.dma_start(bd_sb[:, :], fbd.rearrange("(o d) -> o d", o=1).broadcast_to([B, D])).then_inc(load_c, 16)
            for a in range(2):
                act.dma_start(fwq_sb[:, :, a, :], fWq[:, a * RH * KD:(a + 1) * RH * KD].rearrange("d (h n) -> d h n", h=RH)).then_inc(load_c, 16)
            act.dma_start(key_sb[:, :, :], keys.rearrange("h k p n -> k h (p n)")).then_inc(load_c, 16)
            act.dma_start(down_sb[:, :, :], down.rearrange("(c p) d -> p c d", p=P)).then_inc(load_c, 16)
            act.wait_ge(load_c, 112)
            nc.scalar.activation(c_th[:, :], c_sb[:, :], ACT.Tanh, scale=0.5).then_inc(su_act, 1)

            def body(i, attn, ffn, first):
                w = Work(act, i, attn, ffn)
                w.first_loop = first
                f = i - 1

                def evacuate(dst, src, name, k=0):
                    w.wait_full(name, k)
                    w.release(nc.scalar.copy(dst, src), name, k)

                if attn:
                    evacuate(xT[:, :], w.bank("xT")[:, 0:N], "xT")
                    for p in range(2):
                        evacuate(qk[:, p, :], w.bank("QK", p)[:, :], "QK", p)
                    for n in range(2 * TB):
                        k, half = divmod(n, 2)
                        evacuate(v[:, k, half * 8:half * 8 + 8, 0:DH],
                                 w.bank("V", n)[:, :].rearrange("p (h d) -> p h d", h=8), "V", n)
                for s in range(NSTEP):
                    if attn and s + 2 < NP:
                        if s + 2 >= 4:
                            act.wait_ge(S(s_full), at(s_full, i, s - 1))
                        evacuate(qk[:, (s + 2) % 4, :], w.bank("QK", s + 2)[:, :], "QK", s + 2)
                    if attn and 1 <= s <= NP:
                        p = s - 1
                        act.wait_ge(S(t_full), at(t_full, i, p + 1))
                        if p >= 2:
                            w.wait_full("PV", p - 2)
                        nc.scalar.activation(pT[:, p % 2], pTT[:, :, 0:SW], ACT.Exp, scale=SCALE).then_inc(S(exp_done), 1)
                    if ffn:
                        if s == 1:
                            evacuate(h2T[:, :], w.bank("hT")[:, 0:N], "hT")
                        if s == 2:
                            for k in range(TB):
                                evacuate(sim[:, k].rearrange("p a h n -> p (a h n)"), w.bank("sim", k)[:, :], "sim", k)
                        if 3 <= s < 3 + FC:
                            c = s - 3
                            w.wait_full("GU", c)
                            bank = w.bank("GU", c)
                            nc.scalar.activation(g_t[:, c, :], bank[:, 0:N], ACT.Tanh, bias=b_gh[:, c:c + 1], scale=0.5)
                            nc.scalar.activation(u_sb[:, c, :], bank[:, N:2 * N], ACT.Identity,
                                                 bias=b_u[:, c:c + 1]).then_inc(S(gu_act), 1)
                        if s == 5:
                            act.wait_ge(S(top_ready), at(top_ready, f, 1))
                            nc.scalar.activation(e8[:, :, :, :], top8[:, :, :, :], ACT.Exp).then_inc(S(e8_ready), 1)
                        if s in (5, 6):
                            k = s - 5
                            act.wait_ge(S(f_ready), at(f_ready, f, k + 1))
                            nc.scalar.activation(fexp[:, k].rearrange("p h e -> p (h e)"),
                                                 fsum[:, k].rearrange("p h i j -> p (h i j)"), ACT.Exp).then_inc(S(fexp_ready), 1)
                        if s in (7, 8):
                            k = s - 7
                            w.wait_full("D", k)
                            nc.scalar.activation(d_t[:, k, :], w.bank("D", k)[:, :], ACT.Tanh, scale=0.5).then_inc(S(d_act), 1)
                        if s in (9, 10):
                            k = s - 9
                            evacuate(eT[:, k].rearrange("p c t -> p (c t)"), w.bank("ET", k)[:, :], "ET", k)
                    if attn and s == 2:
                        w.wait_full("PV", 0)
                        nc.scalar.activation(g_th[:, :, :].rearrange("p k h -> p (k h)"), w.bank("PV", 0)[:, 320:320 + TB * H],
                                             ACT.Tanh, scale=0.5).then_inc(S(gate_done), 1)
                    if attn and 3 <= s < NP + 3:
                        evacuate(aoT[:, s - 3, :], w.bank("AO", s - 3)[:, 0:N], "AO", s - 3)

            act.wait_ge(su_pe, 2)
            nc.scalar.copy(fwqT[:, :], pS[0][:, 0, :]).then_inc(su_act, 1)
            act.wait_ge(su_pe, 3)
            nc.scalar.copy(keyT[:, :], pS[0][:, 1, 0:RH * NK]).then_inc(su_act, 1)
            act.wait_ge(su_pe, 4)
            nc.scalar.copy(w_down[:, :], pS[1][:, 0, :]).then_inc(su_act, 1)
            act.wait_ge(su_pe, 5)
            nc.scalar.copy(w_sim[:, 0:RH * NK], pTT[:, 0, 0:RH * NK])
            nc.scalar.copy(w_sim[:, RH * NK:2 * RH * NK], pTT[:, 1, 0:RH * NK]).then_inc(su_act, 1)
            run(act, body)

        @block.vector
        def _(dve):
            n_links = {ln1_chain: 0, attn_chain: 0, ffn_chain: 0}

            def link(ins, chain, b):
                n_links[chain] += 1
                ins.then_inc(S(chain), 1)
                dve.wait_ge(S(chain), at(chain, b, n_links[chain]))

            def apart():
                dve.nop(nofuse=True)

            def done(chain):
                assert n_links[chain] == per[chain][1], (chain, n_links[chain])
                n_links[chain] = 0

            su = [0]

            def su_link(ins):
                su[0] += 1
                ins.then_inc(su_dve, 1)
                dve.wait_ge(su_dve, su[0])

            dve.wait_ge(load_c, 112)
            dve.wait_ge(su_act, 1)
            su_link(nc.vector.scalar_tensor_tensor(out=c_silu[:, :], in0=c_th[:, :], scalar=1.0, in1=c_sb[:, :], op0=ALU.add, op1=ALU.mult))
            su_link(nc.vector.tensor_scalar(c_silu[:, :], c_silu[:, :], 0.5, None, ALU.mult))
            dve.wait_ge(su_pe, 1)
            su_link(nc.vector.tensor_copy(cT[:, :], pW[0][:, 0:B]))
            dve.wait_ge(load_qkv, 64)
            nc.vector.tensor_scalar(w_qkv[:, :], w_qkv[:, :], nw[:, 0:1], None, ALU.mult)
            nc.vector.tensor_scalar(w_gate[:, :], w_gate[:, :], nw[:, 0:1], None, ALU.mult)
            dve.wait_ge(load_w, 112)
            nc.vector.tensor_scalar(w_out[:, :, :], w_out[:, :, :], 0.5, None, ALU.mult)
            nc.vector.tensor_scalar(w_d[:, :, :], w_d[:, :, :], 0.5, None, ALU.mult)
            nc.vector.tensor_scalar(w_up[:, :, :], w_up[:, :, :], 0.5, None, ALU.mult)
            nc.vector.tensor_scalar(b_gh[:, :], b_g[:, :], 0.5, None, ALU.mult).then_inc(const_dve, 1)
            dve.wait_ge(su_pe, 6)
            nc.vector.tensor_copy(mod_sb[:, 0:BANK], pW[0][0:B, :])
            su_link(nc.vector.tensor_copy(mod_sb[:, BANK:6 * D], pW[1][0:B, 0:6 * D - BANK]))
            m6 = mod_sb[:, :].rearrange("b (m d) -> b m d", m=6)
            gates = m6[:, 2:6:3, :]
            nc.vector.tensor_copy(mods[:, SA, :], m6[:, 0, :])
            nc.vector.tensor_scalar(mods[:, CA, :], m6[:, 1, :], 1.0, None, ALU.add)
            nc.vector.tensor_copy(mods[:, SB, :], m6[:, 3, :])
            nc.vector.tensor_scalar(mods[:, CB, :], m6[:, 4, :], 1.0, None, ALU.add)
            nc.vector.tensor_scalar(sgn[:, :, :], gates, 0.0, 2.0, ALU.is_ge, ALU.mult)
            su_link(nc.vector.scalar_tensor_tensor(out=mag[:, :, :], in0=gates, scalar=-1.0, in1=gates, op0=ALU.mult, op1=ALU.max))
            su_link(nc.vector.tensor_scalar(sgn[:, :, :], sgn[:, :, :], -1.0, None, ALU.add))
            su_link(nc.vector.scalar_tensor_tensor(out=mods[:, GA:GB + 1, :], in0=mag[:, :, :], scalar=0.25, in1=sgn[:, :, :],
                                                   op0=ALU.max, op1=ALU.mult))
            su_link(nc.vector.tensor_tensor(mods[:, GD, :], mods[:, GB, :], bd_sb[:, :], ALU.mult))

            def ln1_stats(b):
                dve.wait_ge(S(x_loaded), at(x_loaded, b, 16))
                for k in range(TB):
                    ins = nc.vector.bn_stats(st1[:, k, :], x_in[:, k, :])
                link(ins, ln1_chain, b)
                apart()
                for k in range(TB):
                    ins = nc.vector.bn_aggr(mv1[:, k, :], st1[:, k, :])
                ins.then_inc(S(rstd1_in), 1)

            def ln1_modulate(b):
                dve.wait_ge(S(rstd1_out), at(rstd1_out, b, 1))
                dve.wait_ge(S(modA_loaded), at(modA_loaded, b, 16))
                for k in range(TB):
                    ins = nc.vector.tensor_scalar(h1[:, k, :], x_in[:, k, :], mv1[:, k, 0:1], rs1[:, k:k + 1], ALU.subtract, ALU.mult)
                link(ins, ln1_chain, b)
                link(nc.vector.tensor_tensor(h1[:, :, :], h1[:, :, :], modA[:, 1:2, :].broadcast_to([P, TB, D]), ALU.mult), ln1_chain, b)
                link(nc.vector.tensor_tensor(h1[:, :, :], h1[:, :, :], modA[:, 0:1, :].broadcast_to([P, TB, D]), ALU.add), ln1_chain, b)
                for k in range(TB):
                    ins = nc.vector.tensor_tensor_reduce(out=sq1[:, k, :], in0=h1[:, k, :], in1=h1[:, k, :], scale=1.0, scalar=0.0,
                                                         op0=ALU.mult, op1=ALU.add, accum_out=ms1[:, k:k + 1])
                ins.then_inc(S(rstd1_in), 1)

            def ln1_rms(b):
                dve.wait_ge(S(rstd1_out), at(rstd1_out, b, 2))
                for k in range(TB):
                    ins = nc.vector.tensor_scalar(xr[:, k, :], h1[:, k, :], rr1[:, k:k + 1], None, ALU.mult)
                ins.then_inc(S(xr_ready), 1)
                done(ln1_chain)

            ln1_stats(0)
            ln1_modulate(0)
            ln1_rms(0)

            def body(i, attn, ffn, first):
                w = Work(dve, i, attn, ffn)
                w.first_loop = first
                f = i - 1
                ahead = attn and not (isinstance(i, int) and i + 1 >= B)
                if ffn:
                    w.wait_full("op")
                    dve.wait_ge(S(res_loaded), at(res_loaded, f, 16))
                    dve.wait_ge(S(modB_loaded), at(modB_loaded, f, 16))
                    ins = nc.vector.tensor_tensor(ga_o[:, :, :], w.bank("op")[:, 0:N].rearrange("p (k d) -> p k d", k=TB),
                                                  modB[:, 2:3, :].broadcast_to([P, TB, D]), ALU.mult)
                    w.release(ins, "op")
                    dve.wait_ge(S(work_free[w.key("op", 0)]), at(work_free[w.key("op", 0)], f, place["op", 0] + 1))
                    ins = nc.vector.tensor_tensor(x2[:, :, :], ga_o[:, :, :], x_res[:, :, :], ALU.add)
                    ins.then_inc(S(x2_ready), 1)
                    dve.wait_ge(S(x2_ready), at(x2_ready, f, 1))
                    for k in range(TB):
                        ins = nc.vector.bn_stats(st2[:, k, :], x2[:, k, :])
                    link(ins, ffn_chain, f)
                    apart()
                    for k in range(TB):
                        ins = nc.vector.bn_aggr(mv2[:, k, :], st2[:, k, :])
                    ins.then_inc(S(rstd2_in), 1)
                for s in range(NSTEP):
                    if attn and s < NP:
                        slot = s % 2
                        dve.wait_ge(S(s_full), at(s_full, i, s + 1))
                        nc.vector.reduce_max(mx[:, slot, :, 0], pS[slot][:, :, 0:P], AX_X)
                        link(nc.vector.reduce_max(mx[:, slot, :, 1], pS[slot][:, :, P:SW], AX_X), attn_chain, i)
                        if s >= 2:
                            dve.wait_ge(S(t_full), at(t_full, i, s - 1))
                        nc.vector.tensor_tensor(s_sb[:, slot, :, 0:P], pS[slot][:, :, 0:P],
                                                mx[:, slot, :, 0:1].broadcast_to([P, 2, P]), ALU.subtract)
                        nc.vector.tensor_tensor(s_sb[:, slot, :, P:SW], pS[slot][:, :, P:SW],
                                                mx[:, slot, :, 1:2].broadcast_to([P, 2, SW - P]), ALU.subtract).then_inc(S(s_taken), 1)
                    if ffn:
                        if s == 0:
                            dve.wait_ge(S(rstd2_out), at(rstd2_out, f, 1))
                            for k in range(TB):
                                ins = nc.vector.tensor_scalar(h2[:, k, :], x2[:, k, :], mv2[:, k, 0:1], rs2[:, k:k + 1], ALU.subtract, ALU.mult)
                            link(ins, ffn_chain, f)
                            link(nc.vector.tensor_tensor(h2[:, :, :], h2[:, :, :], modB[:, 1:2, :].broadcast_to([P, TB, D]), ALU.mult), ffn_chain, f)
                            nc.vector.tensor_tensor(h2[:, :, :], h2[:, :, :], modB[:, 0:1, :].broadcast_to([P, TB, D]), ALU.add).then_inc(S(h2_ready), 1)
                        if s == 3 or s == 4:
                            k = s - 3
                            e = work_free[w.key("sim", k)]
                            dve.wait_ge(S(e), at(e, f, place["sim", k] + 1))
                            apart()
                            for a in range(2):
                                for h in range(RH):
                                    ins = nc.vector.max(tops[:, a, k, h, :], sim[:, k, a, h, :])
                            if k == TB - 1:
                                link(ins, ffn_chain, f)
                                link(nc.vector.tensor_tensor(big[:, :, :, :], tops[:, 0, :, :, 0:1], tops[:, 1, :, :, 0:1], ALU.add), ffn_chain, f)
                                nc.vector.tensor_tensor(xs[:, :, :, :], sim[:, :, 0, :, 0:NX], big[:, :, :, :].broadcast_to([P, TB, RH, NX]),
                                                        ALU.subtract).then_inc(S(xs_ready), 1)
                                link(nc.vector.tensor_tensor(sx[:, :, :, :], tops[:, 0], big[:, :, :, :].broadcast_to([P, TB, RH, TK]),
                                                             ALU.subtract), ffn_chain, f)
                                link(nc.vector.tensor_tensor(
                                    cand[:, :, :, :, :].rearrange("p k h a b -> p (k h) a b"),
                                    sx[:, :, :, :].rearrange("p k h a -> p (k h) a").unsqueeze(3).broadcast_to([P, TB * RH, TK, TK]),
                                    tops[:, 1].rearrange("p k h a -> p (k h) a").unsqueeze(2).broadcast_to([P, TB * RH, TK, TK]),
                                    ALU.add), ffn_chain, f)
                                apart()
                                for kk in range(TB):
                                    for h in range(RH):
                                        ins = nc.vector.max(top8[:, kk, h, :], cand[:, kk, h].rearrange("p a b -> p (a b)"))
                                ins.then_inc(S(top_ready), 1)
                        if s == 5:
                            dve.wait_ge(S(e8_ready), at(e8_ready, f, 1))
                            link(nc.vector.reduce_sum(zz[:, :, :], e8[:, :, :, :], AX_X), ffn_chain, f)
                            link(nc.vector.reciprocal(rz[:, :, :], zz[:, :, :]), ffn_chain, f)
                        if s in (6, 7):
                            k = s - 6
                            dve.wait_ge(S(fexp_ready), at(fexp_ready, f, k + 1))
                            for h in range(RH):
                                ins = nc.vector.scalar_tensor_tensor(
                                    out=fexp[:, k, h, :], in0=fsum[:, k, h].rearrange("p i j -> p (i j)"), scalar=top8[:, k, h, TK - 1:TK],
                                    in1=fexp[:, k, h, :], op0=ALU.is_ge, op1=ALU.mult)
                            link(ins, ffn_chain, f)
                            link(nc.vector.tensor_scalar(wsum[:, k, :], fexp[:, k, 0, :], rz[:, k, 0:1], None, ALU.mult), ffn_chain, f)
                            for h in range(1, RH - 1):
                                link(nc.vector.scalar_tensor_tensor(out=wsum[:, k, :], in0=fexp[:, k, h, :], scalar=rz[:, k, h:h + 1],
                                                                    in1=wsum[:, k, :], op0=ALU.mult, op1=ALU.add), ffn_chain, f)
                            h = RH - 1
                            link(nc.vector.scalar_tensor_tensor(out=wsum[:, k, :], in0=fexp[:, k, h, :], scalar=rz[:, k, h:h + 1],
                                                                in1=wsum[:, k, :], op0=ALU.mult, op1=ALU.add,
                                                                accum_out=tot[:, k:k + 1]), ffn_chain, f)
                            link(nc.vector.tensor_scalar(tot[:, k:k + 1], tot[:, k:k + 1], -1.0, float(RH), ALU.mult, ALU.add), ffn_chain, f)
                            nc.vector.tensor_tensor(wsum[:, k, NE - 1:NE], wsum[:, k, NE - 1:NE], tot[:, k:k + 1],
                                                    ALU.add).then_inc(S(wsum_ready), 1)
                        if 3 <= s < 3 + FC:
                            c = s - 3
                            dve.wait_ge(S(gu_act), at(gu_act, f, c + 1))
                            w.release(nc.vector.scalar_tensor_tensor(out=gu[:, c, :], in0=w.bank("GU", c)[:, 0:N], scalar=b_g[:, c:c + 1],
                                                                     in1=u_sb[:, c, :], op0=ALU.add, op1=ALU.mult), "GU", c)
                        if s in (7, 8):
                            k = s - 7
                            dve.wait_ge(S(d_act), at(d_act, f, k + 1))
                            ins = nc.vector.scalar_tensor_tensor(out=d_s[:, k, :], in0=d_t[:, k, :], scalar=1.0, in1=w.bank("D", k)[:, :],
                                                                 op0=ALU.add, op1=ALU.mult)
                            w.release(ins, "D", k)
                        if s == 8:
                            nc.vector.scalar_tensor_tensor(out=m_sb[:, :, :].rearrange("p c t -> p (c t)"), in0=g_t[:, :, :].rearrange("p c t -> p (c t)"),
                                                           scalar=1.0, in1=gu[:, :, :].rearrange("p c t -> p (c t)"),
                                                           op0=ALU.add, op1=ALU.mult).then_inc(S(gu_ready), 1)
                    if attn and 2 <= s < NP + 2:
                        p = s - 2
                        if p == 0:
                            dve.wait_ge(S(gate_done), at(gate_done, i, 1))
                        w.wait_full("PV", p)
                        pv = w.bank("PV", p)[:, 0:2 * TB * (DH + 1)].rearrange("p (h k e) -> p h k e", h=2, k=TB)
                        link(nc.vector.reciprocal(rden[:, :, :], pv[:, :, :, DH]), attn_chain, i)
                        link(nc.vector.scalar_tensor_tensor(out=coef[:, :, :], in0=g_th[:, :, 2 * p:2 * p + 2].rearrange("p k h -> p h k"),
                                                            scalar=1.0, in1=rden[:, :, :], op0=ALU.add, op1=ALU.mult), attn_chain, i)
                        if p >= 2:
                            e = work_full[w.key("AO", p - 2)]
                            dve.wait_ge(S(e), at(e, i, place["AO", p - 2] + 1))
                        ins = nc.vector.tensor_tensor(ao[:, p % 2].rearrange("p k (h d) -> p h k d", h=2), pv[:, :, :, 0:DH],
                                                      coef[:, :, :].unsqueeze(3).broadcast_to([P, 2, TB, DH]), ALU.mult)
                        w.release(ins, "PV", p)
                    if ahead:
                        if s == 1:
                            ln1_stats(i + 1)
                        if s == 2:
                            ln1_modulate(i + 1)
                        if s == 3:
                            ln1_rms(i + 1)
                if ffn:
                    w.wait_full("y")
                    dve.wait_ge(S(modC_loaded), at(modC_loaded, f, 16))
                    ins = nc.vector.tensor_tensor(y_g[:, :, :], w.bank("y")[:, 0:N].rearrange("p (k d) -> p k d", k=TB),
                                                  modC[:, 0:1, :].broadcast_to([P, TB, D]), ALU.mult)
                    w.release(ins, "y")
                    e = work_free[w.key("y", 0)]
                    dve.wait_ge(S(e), at(e, f, place["y", 0] + 1))
                    dve.wait_ge(S(x2g_ready), at(x2g_ready, f, 1))
                    if not first:
                        dve.wait_ge(S(out_stored), at(out_stored, f, 0))
                    nc.vector.tensor_tensor(yo[:, :, :], y_g[:, :, :], x2g[:, :, :], ALU.add).then_inc(S(yo_ready), 1)
                    done(ffn_chain)
                if attn:
                    done(attn_chain)

            run(dve, body)

        @block.tensor
        def _(pe):
            mm, tp = nc.tensor.matmul, nc.tensor.transpose
            pe.wait_ge(const_pool, 2)
            pe.wait_ge(su_dve, 2)
            tp(pW[0][:, 0:B], c_silu[:, :], ident[0:B, 0:B]).then_inc(su_pe, 1)
            pe.wait_ge(load_c, 112)
            for h in range(RH):
                ins = tp(pS[0][:, 0, h * D:(h + 1) * D], fwq_sb[:, h].rearrange("d p n -> d (p n)"), ident[:, :])
            ins.then_inc(su_pe, 1)
            for h in range(RH):
                ins = tp(pS[0][:, 1, h * NK:(h + 1) * NK], key_sb[:, h, :], ident[0:NK, 0:NK])
            ins.then_inc(su_pe, 1)
            for c in range(EC):
                ins = tp(pS[1][:, 0, c * P:(c + 1) * P], down_sb[:, c, :], ident[:, :])
            ins.then_inc(su_pe, 1)
            pe.wait_ge(su_act, 3)
            for a in range(2):
                rows = slice(a * KD, (a + 1) * KD)
                for h in range(RH):
                    ins = mm(pTT[:, a, h * NK:(h + 1) * NK], fwqT[rows, h * D:(h + 1) * D], keyT[rows, h * NK:(h + 1) * NK],
                             start=True, stop=True)
            ins.then_inc(su_pe, 1)
            pe.wait_ge(su_dve, 3)
            mm(pW[0][0:B, :], cT[:, :], wmod_sb[:, 0:BANK], start=True, stop=True)
            mm(pW[1][0:B, 0:6 * D - BANK], cT[:, :], wmod_sb[:, BANK:6 * D], start=True, stop=True).then_inc(su_pe, 1)
            pe.wait_ge(su_act, 5)
            pe.wait_ge(su_dve, 4)
            pe.wait_ge(const_dve, 1)

            def body(i, attn, ffn, first):
                w = Work(pe, i, attn, ffn)
                w.first_loop = first
                f = i - 1

                def released(name, k=0):
                    e = work_free[w.key(name, k)]
                    pe.wait_ge(S(e), at(e, w.batch(name, k), place[name, k] + 1))

                def project_qk(p):
                    w.wait_free("QK", p)
                    bank = w.bank("QK", p)
                    mm(bank[:, 0:N], w_qkv[:, p * P:(p + 1) * P], xT[:, :], start=True, stop=True)
                    w.filled(mm(bank[:, N:2 * N], w_qkv[:, DI + p * P:DI + (p + 1) * P], xT[:, :], start=True, stop=True), "QK", p)

                def project_v(n):
                    k, half = divmod(n, 2)
                    w.wait_free("V", n)
                    w.filled(mm(w.bank("V", n)[:, :], xT[:, k * P:(k + 1) * P], w_qkv[:, 2 * DI + half * BANK:2 * DI + (half + 1) * BANK],
                                start=True, stop=True), "V", n)

                def scores(p):
                    released("QK", p)
                    if p >= 2:
                        pe.wait_ge(S(s_taken), at(s_taken, i, p - 1))
                    elif not (isinstance(i, int) and i == 0):
                        pe.wait_ge(S(s_taken), at(s_taken, i - 1, NP - 1 + p))
                    ps = pS[p % 2]
                    for h in range(2):
                        r = slice(h * DH, (h + 1) * DH)
                        mm(ps[:, h, 0:P], qk[r, p % 4, 0:P], qk[r, p % 4, N:N + P], start=True, stop=False, skip_group_check=True)
                    for h in range(2):
                        r = slice(h * DH, (h + 1) * DH)
                        mm(ps[:, h, P:SW], qk[r, p % 4, P:N], qk[r, p % 4, N:2 * N], start=False, stop=False, skip_group_check=True)
                    for h in range(2):
                        mm(ps[:, h, 0:P], ident_bf[:, :], mask[:, :], start=False, stop=True, skip_group_check=True)
                        ins = mm(ps[:, h, 2 * P:SW], ident_bf[:, :], mask[:, :], start=False, stop=True, skip_group_check=True)
                    ins.then_inc(S(s_full), 1)

                def transpose_scores(p):
                    pe.wait_ge(S(s_taken), at(s_taken, i, p + 1))
                    if p >= 1:
                        pe.wait_ge(S(exp_done), at(exp_done, i, p))
                    elif not (isinstance(i, int) and i == 0):
                        pe.wait_ge(S(exp_done), at(exp_done, i, 0))
                    for h in range(2):
                        for b in range(BLOCKS):
                            ins = tp(pTT[:, h, b * P:(b + 1) * P], s_sb[:, p % 2, h, b * P:(b + 1) * P], ident[:, :])
                    ins.then_inc(S(t_full), 1)

                def weigh_values(p):
                    if p == 0:
                        released("V", 2 * TB - 1)
                    pe.wait_ge(S(exp_done), at(exp_done, i, p + 1))
                    w.wait_free("PV", p)
                    bank = w.bank("PV", p)
                    E1 = DH + 1
                    for h in range(2):
                        hh = 2 * p + h
                        o0, o1 = (2 * h) * E1, (2 * h + 1) * E1
                        mm(bank[:, o0:o0 + E1], pT[:, p % 2, h, 0:P], v[:, 0, hh, :], start=True, stop=True)
                        mm(bank[:, o1:o1 + E1], pT[:, p % 2, h, P:2 * P], v[:, 0, hh, :], start=True, stop=False)
                        ins = mm(bank[:, o1:o1 + E1], pT[:, p % 2, h, 2 * P:3 * P], v[:, 1, hh, :], start=False, stop=True)
                    if p == 0:
                        for k in range(TB):
                            ins = mm(bank[:, 320 + k * H:320 + (k + 1) * H], xT[:, k * P:(k + 1) * P], w_gate[:, :], start=True, stop=True)
                    w.filled(ins, "PV", p)

                def transpose_out(p):
                    released("PV", p)
                    w.wait_free("AO", p)
                    for k in range(TB):
                        ins = tp(w.bank("AO", p)[:, k * P:(k + 1) * P], ao[:, p % 2, k, :], ident[:, :])
                    w.filled(ins, "AO", p)

                def second_half(step):
                    if step == 1:
                        pe.wait_ge(S(h2_ready), at(h2_ready, f, 1))
                        w.wait_free("hT")
                        for k in range(TB):
                            ins = tp(w.bank("hT")[:, k * P:(k + 1) * P], h2[:, k, :], ident[:, :])
                        w.filled(ins, "hT")
                    if step == 2:
                        released("hT")
                        for k in range(TB):
                            w.wait_free("sim", k)
                            w.filled(mm(w.bank("sim", k)[:, :], h2T[:, k * P:(k + 1) * P], w_sim[:, :], start=True, stop=True), "sim", k)
                    if 3 <= step < 3 + FC:
                        c = step - 3
                        w.wait_free("GU", c)
                        bank = w.bank("GU", c)
                        mm(bank[:, 0:N], w_g[:, c * P:(c + 1) * P], h2T[:, :], start=True, stop=True)
                        w.filled(mm(bank[:, N:2 * N], w_u[:, c * P:(c + 1) * P], h2T[:, :], start=True, stop=True), "GU", c)
                    if step in (7, 8):
                        k = step - 7
                        w.wait_free("D", k)
                        w.filled(mm(w.bank("D", k)[:, :], h2T[:, k * P:(k + 1) * P], w_down[:, :], start=True, stop=True), "D", k)
                    if step in (9, 10):
                        k = step - 9
                        pe.wait_ge(S(eo_ready), at(eo_ready, f, k + 1))
                        w.wait_free("ET", k)
                        for c in range(EC):
                            ins = tp(w.bank("ET", k)[:, c * P:(c + 1) * P], eo[:, k, c * P:(c + 1) * P], ident[:, :])
                        w.filled(ins, "ET", k)

                if attn:
                    pe.wait_ge(S(xr_ready), at(xr_ready, i, 1))
                    w.wait_free("xT")
                    for k in range(TB):
                        ins = tp(w.bank("xT")[:, k * P:(k + 1) * P], xr[:, k, :], ident[:, :])
                    w.filled(ins, "xT")
                if ffn:
                    e = work_free[bank_of["AO", NP - 1], "a"]
                    pe.wait_ge(S(e), at(e, f, place["AO", NP - 1] + 1))
                    w.wait_free("op")
                    for k in range(TB):
                        for p in range(NP):
                            ins = mm(w.bank("op")[:, k * D:(k + 1) * D], aoT[:, p, k * P:(k + 1) * P], w_out[:, p, :],
                                     start=p == 0, stop=p == NP - 1)
                    w.filled(ins, "op")
                if attn:
                    released("xT")
                    project_qk(0)
                    project_qk(1)
                    for n in range(2 * TB):
                        project_v(n)
                for s in range(NSTEP):
                    if attn and s + 2 < NP:
                        project_qk(s + 2)
                    if attn and s < NP:
                        scores(s)
                    if attn and 1 <= s <= NP:
                        transpose_scores(s - 1)
                    if ffn:
                        second_half(s)
                    if attn and 2 <= s < NP + 2:
                        weigh_values(s - 2)
                    if attn and 3 <= s < NP + 3:
                        transpose_out(s - 3)
                if ffn:
                    pe.wait_ge(S(gu_ready), at(gu_ready, f, 1))
                    released("ET", TB - 1)
                    w.wait_free("y")
                    for k in range(TB):
                        o = w.bank("y")[:, k * D:(k + 1) * D]
                        for c in range(FC):
                            mm(o, m_sb[:, c, k * P:(k + 1) * P], w_d[:, c, :], start=c == 0, stop=False)
                        for c in range(EC):
                            ins = mm(o, eT[:, k, c, :], w_up[:, c, :], start=False, stop=c == EC - 1)
                    w.filled(ins, "y")

            run(pe, body)


LN1_LINKS, ATTN_LINKS, FFN_LINKS, SU_LINKS = 4, 24, 21, 8

_INS = ['L0_attn_tokens', 'L0_attn_norm_w', 'L0_attn_Wq', 'L0_attn_Wkv', 'L0_attn_Wout', 'L0_attn_Wg', 'L0_ffn_Wg',
        'L0_ffn_bg', 'L0_ffn_Wu', 'L0_ffn_bu', 'L0_ffn_Wd', 'L0_ffn_bd', 'L0_ffn_Wq', 'L0_ffn_keys', 'L0_ffn_down_embed',
        'L0_ffn_up_embed', 'L0_c', 'L0_wmod']


def kernel(**inputs):
    import numpy as _np
    import concourse.bacc as _bacc
    from concourse import mybir as _mybir
    from concourse.bass_utils import run_bass_kernel_spmd as _run

    nc = _bacc.Bacc("TRN2", target_bir_lowering=False, num_devices=1)
    arrays, args = {}, []
    for name in _INS:
        a = _np.ascontiguousarray(inputs[name])
        arrays[f"in_{name}"] = a
        args.append(nc.dram_tensor(f"in_{name}", a.shape, _mybir.dt.from_np(a.dtype), kind="ExternalInput").ap())
    out = nc.dram_tensor("out", (B, N, D), _mybir.dt.float32, kind="ExternalOutput").ap()
    program(nc, *args, out)
    r = _run(nc, [arrays], core_ids=[0])
    return r.results[0]["out"]
```

```python
import concourse.bass as bass
from concourse import mybir
from contextlib import ExitStack

F32 = mybir.dt.float32
BF16 = mybir.dt.bfloat16
ALU = mybir.AluOpType
ACT = mybir.ActivationFunctionType
AX_X = mybir.AxisListType.X

B, N, D = 32, 256, 128
P = 128
TB = N // P
H, DH = 16, 64
NP = H // 2
DI = H * DH
BLOCKS = TB * (TB + 1) // 2
SW = BLOCKS * P
F = 512
FC = F // P
NE = 512
EC = NE // P
RH, NK, KD, TK = 4, 64, 64, 8
NX = NE // NK
SCALE = float(DH) ** -0.5
LN_EPS = 1e-5
RMS_EPS = 2.0 ** -23
MASKED = -1e30
NSTEP = NP + 2
NW = 4
BANK = 512
ET_BLOCK = (1, 0)
NMOD = 7
SA, CA, SB, CB, GA, GB, GD = range(NMOD)


def program(nc, x, norm_w, Wq, Wkv, Wout, Wgate, fWg, fbg, fWu, fbu, fWd, fbd, fWq, keys,
            down, up, cond, wmod, out):
    ctx = ExitStack()
    with ctx:
        def sb(name, shape, dt=F32):
            return ctx.enter_context(nc.sbuf_tensor(name, shape, dt))

        def sem(name):
            return ctx.enter_context(nc.semaphore(name))

        ident = sb("ident", [P, P])
        ident_bf = sb("ident_bf", [P, P], BF16)
        mask = sb("mask", [P, P], BF16)
        expo = sb("expo", [P, TB])
        w_qkv = sb("w_qkv", [P, 3 * DI])
        w_gate = sb("w_gate", [P, H])
        nw = sb("nw", [P, 1])
        w_out = sb("w_out", [P, NP, D])
        w_g = sb("w_g", [P, F])
        w_u = sb("w_u", [P, F])
        b_g = sb("b_g", [P, FC])
        b_gh = sb("b_gh", [P, FC])
        b_u = sb("b_u", [P, FC])
        w_d = sb("w_d", [P, FC, D])
        w_up = sb("w_up", [P, EC, D])
        w_down = sb("w_down", [P, NE])
        w_sim = sb("w_sim", [P, 2 * RH * NK])

        fwq_sb = sb("fwq_sb", [P, RH, 2, KD])
        fwqT = sb("fwqT", [P, RH * D])
        key_sb = sb("key_sb", [NK, RH, 2 * KD])
        keyT = sb("keyT", [P, RH * NK])
        down_sb = sb("down_sb", [P, EC, D])
        c_sb = sb("c_sb", [B, D])
        c_th = sb("c_th", [B, D])
        c_silu = sb("c_silu", [B, D])
        cT = sb("cT", [P, B])
        wmod_sb = sb("wmod_sb", [P, 6 * D])
        mod_sb = sb("mod_sb", [B, 6 * D])
        mods = sb("mods", [B, NMOD, D])
        sgn = sb("sgn", [B, 2, D])
        mag = sb("mag", [B, 2, D])
        bd_sb = sb("bd_sb", [B, D])
        mods_dram = nc.dram_tensor("mods_dram", [B, NMOD * D], F32, kind="Internal").ap()

        x_in = sb("x_in", [P, TB, D])
        x_res = sb("x_res", [P, TB, D])
        modA = sb("modA", [P, 2, D])
        modB = sb("modB", [P, 3, D])
        modC = sb("modC", [P, 2, D])
        st1 = sb("st1", [P, TB, 6])
        mv1 = sb("mv1", [P, TB, 2])
        ve1 = sb("ve1", [P, TB])
        rs1 = sb("rs1", [P, TB])
        h1 = sb("h1", [P, TB, D])
        sq1 = sb("sq1", [P, TB, D])
        ms1 = sb("ms1", [P, TB])
        me1 = sb("me1", [P, TB])
        rr1 = sb("rr1", [P, TB])
        xr = sb("xr", [P, TB, D])
        xT = sb("xT", [P, N])
        qk = sb("qk", [P, 4, 2 * N])
        v = sb("v", [P, TB, H, DH + 1])
        s_sb = sb("s_sb", [P, 2, 2, SW])
        mx = sb("mx", [P, 2, 2, TB])
        pT = sb("pT", [P, 2, 2, SW])
        g_th = sb("g_th", [P, TB, H])
        rden = sb("rden", [P, 2, TB])
        coef = sb("coef", [P, 2, TB])
        ao = sb("ao", [P, 2, TB, P])
        aoT = sb("aoT", [P, NP, N])
        ga_o = sb("ga_o", [P, TB, D])
        x2 = sb("x2", [P, TB, D])
        x2g = sb("x2g", [P, TB, D])
        st2 = sb("st2", [P, TB, 6])
        mv2 = sb("mv2", [P, TB, 2])
        ve2 = sb("ve2", [P, TB])
        rs2 = sb("rs2", [P, TB])
        h2 = sb("h2", [P, TB, D])
        h2T = sb("h2T", [P, N])
        sim = sb("sim", [P, TB, 2, RH, NK])
        tops = sb("tops", [P, 2, TB, RH, TK])
        sxy = sb("sxy", [P, 2, TB, RH, TK])
        xs = sb("xs", [P, TB, RH, NX])
        ys = sb("ys", [P, TB, RH, NK])
        cand = sb("cand", [P, TB, RH, TK, TK])
        top8 = sb("top8", [P, TB, RH, TK])
        e8 = sb("e8", [P, TB, RH, TK])
        zz = sb("zz", [P, TB, RH])
        rz = sb("rz", [P, TB, RH])
        fsum = sb("fsum", [P, TB, RH, NX, NK])
        fexp = sb("fexp", [P, TB, RH, NE])
        chosen = sb("chosen", [P, RH, NE])
        junk = sb("junk", [P, NE])
        ws2 = sb("ws2", [P, 2, NE])
        wsum = sb("wsum", [P, TB, NE])
        tot = sb("tot", [P, TB])
        u_sb = sb("u_sb", [P, FC, N])
        g_t = sb("g_t", [P, FC, N])
        gu = sb("gu", [P, FC, N])
        m_sb = sb("m_sb", [P, FC, N])
        d_t = sb("d_t", [P, TB, NE])
        d_s = sb("d_s", [P, TB, NE])
        eo = sb("eo", [P, TB, NE])
        eT = sb("eT", [P, TB, EC, P])
        y_g = sb("y_g", [P, TB, D])
        yo = sb("yo", [P, TB, D])

        pS = ctx.enter_context(nc.psum_tensor("pS", [P, 2, BANK], F32))
        pTT = ctx.enter_context(nc.psum_tensor("pTT", [P, 2, BANK], F32))
        pW = [ctx.enter_context(nc.psum_tensor(f"pW{n}", [P, BANK], F32)) for n in range(NW)]

        load_qkv, load_w, load_c = sem("load_qkv"), sem("load_w"), sem("load_c")
        const_pool, const_dve = sem("const_pool"), sem("const_dve")
        su_pe, su_act, su_dve = sem("su_pe"), sem("su_act"), sem("su_dve")
        mods_stored = sem("mods_stored")

        per = {}

        def ev(name, n):
            s = sem(name)
            per[name] = (s, n)
            return name

        def at(name, batch, k):
            return batch * per[name][1] + k

        def S(name):
            return per[name][0]

        x_loaded, res_loaded = ev("x_loaded", 16), ev("res_loaded", 16)
        modA_loaded, modB_loaded, modC_loaded = ev("modA_loaded", 16), ev("modB_loaded", 16), ev("modC_loaded", 16)
        out_stored = ev("out_stored", 16)
        ln1_chain, attn_chain, ffn_chain = ev("ln1_chain", LN1_LINKS), ev("attn_chain", ATTN_LINKS), ev("ffn_chain", FFN_LINKS)
        rstd1_in, rstd1_out = ev("rstd1_in", 2), ev("rstd1_out", 2)
        pool_chain1, pool_chain2 = ev("pool_chain1", 2), ev("pool_chain2", 1)
        xr_ready = ev("xr_ready", 1)
        s_full, s_taken = ev("s_full", NP), ev("s_taken", NP)
        t_full, exp_done = ev("t_full", NP), ev("exp_done", NP)

        x2_ready, x2g_ready = ev("x2_ready", 1), ev("x2g_ready", 1)
        rstd2_in, rstd2_out = ev("rstd2_in", 1), ev("rstd2_out", 1)
        h2_ready = ev("h2_ready", 1)
        top_ready, xs_ready = ev("top_ready", 1), ev("xs_ready", 1)
        masks_ready, fexp_ready = ev("masks_ready", 1), ev("fexp_ready", TB)
        f_ready, e8_ready = ev("f_ready", TB), ev("e8_ready", 1)
        pool_sum = ev("pool_sum", 5)
        tot_ready = ev("tot_ready", 1)
        wsum_ready = ev("wsum_ready", 1)
        gu_act, gu_ready = ev("gu_act", FC), ev("gu_ready", 1)
        d_act = ev("d_act", TB)
        eo_ready = ev("eo_ready", TB)
        yo_ready = ev("yo_ready", 1)

        def jobs_of(step):
            js = []
            if step < 0:
                js += [("xT", 0, "a"), ("QK", 0, "a"), ("QK", 1, "a")]
                js += [("op", k, "f") for k in range(TB)]
                return js + [("V", n, "a") for n in range(TB)]
            early = {1: [("hT", 0)], 2: [("D", 0)], 3: [("D", 1), ("GU", 0)], 4: [("GU", 1)],
                     5: [("GU", 2)], 6: [("GU", 3)], 8: [("ET", 0)], 9: [("ET", 1), ("y", 0)]}
            js += [(n, k, "f") for n, k in early.get(step, [])]
            if step == 0:
                js += [("V", n, "a") for n in range(TB, 2 * TB)]
            if step + 2 < NP:
                js.append(("QK", step + 2, "a"))
            if step == 0:
                js.append(("gate", 0, "a"))
            if 1 <= step < NP + 1:
                js.append(("PV", step - 1, "a"))
            if 2 <= step:
                js.append(("AO", step - 2, "a"))
            if step == 1:
                js += [("sim", k, "f") for k in range(TB)]
            return js

        order = [j for step in range(-1, NSTEP) for j in jobs_of(step)]
        assert len(order) % NW == 0, len(order)
        bank_of, place, count = {}, {}, {}
        for n, (name, k, kind) in enumerate(order):
            key = (n % NW, kind)
            bank_of[name, k] = n % NW
            place[name, k] = count.get(key, 0)
            count[key] = place[name, k] + 1
        work_full = {key: ev(f"work_full_{key[1]}{key[0]}", n) for key, n in count.items()}
        work_free = {key: ev(f"work_free_{key[1]}{key[0]}", n) for key, n in count.items()}
        kind_of = {(name, k): kind for name, k, kind in order}

        class Work:

            def __init__(self, eng, i, attn, ffn):
                self.eng, self.i, self.attn, self.ffn = eng, i, attn, ffn

            def key(self, name, k):
                return bank_of[name, k], kind_of[name, k]

            def batch(self, name, k):
                return self.i if kind_of[name, k] == "a" else self.i - 1

            def bank(self, name, k=0):
                return pW[bank_of[name, k]]

            def before(self, name, k):
                mine = [j for j in order if bank_of[j[0], j[1]] == bank_of[name, k]]
                now = [j for j in mine if (self.attn if j[2] == "a" else self.ffn)]
                n = [(j[0], j[1]) for j in now].index((name, k))
                if n:
                    return now[n - 1][:2], self.batch(*now[n - 1][:2])
                if not self.ffn:
                    return None
                j = [j for j in mine if not self.first_loop or j[2] == "a"][-1]
                return j[:2], (self.i if j[2] == "a" else self.i - 1) - 1

            first_loop = False

            def wait_free(self, name, k=0):
                prev = self.before(name, k)
                if prev:
                    (pn, pk), batch = prev
                    ev_ = work_free[self.key(pn, pk)]
                    self.eng.wait_ge(S(ev_), at(ev_, batch, place[pn, pk] + 1))

            def filled(self, ins, name, k=0):
                ins.then_inc(S(work_full[self.key(name, k)]), 1)

            def wait_full(self, name, k=0):
                e = work_full[self.key(name, k)]
                self.eng.wait_ge(S(e), at(e, self.batch(name, k), place[name, k] + 1))

            def release(self, ins, name, k=0):
                ins.then_inc(S(work_free[self.key(name, k)]), 1)

        def run(eng, body):
            body(0, True, False, False)
            body(1, True, True, True)
            with eng.Fori(2, B - 1) as i:
                body(i, True, True, False)
            body(B - 1, True, True, False)
            body(B, False, True, False)

        block = ctx.enter_context(nc.Block())

        @block.sync
        def _(sp):
            sp.dma_start(w_qkv[:, 0:DI], Wq).then_inc(load_qkv, 16)
            sp.dma_start(w_qkv[:, DI:3 * DI], Wkv).then_inc(load_qkv, 16)
            sp.dma_start(w_gate[:, :], Wgate).then_inc(load_qkv, 16)
            sp.dma_start(nw[:, :], norm_w.rearrange("(d o) -> d o", o=1), allow_slow_non_contiguous=True).then_inc(load_qkv, 16)
            sp.dma_start(w_out[:, :, :], Wout.rearrange("(j p) n -> p j n", p=P)).then_inc(load_w, 16)
            sp.dma_start(w_g[:, :], fWg).then_inc(load_w, 16)
            sp.dma_start(w_u[:, :], fWu).then_inc(load_w, 16)
            sp.dma_start(b_g[:, :], fbg.rearrange("(c p) -> p c", p=P), allow_slow_non_contiguous=True).then_inc(load_w, 16)
            sp.dma_start(b_u[:, :], fbu.rearrange("(c p) -> p c", p=P), allow_slow_non_contiguous=True).then_inc(load_w, 16)
            sp.dma_start(w_d[:, :, :], fWd.rearrange("(c p) n -> p c n", p=P)).then_inc(load_w, 16)
            sp.dma_start(w_up[:, :, :], up.rearrange("(c p) n -> p c n", p=P)).then_inc(load_w, 16)

            def load_next(b):
                sp.dma_start(x_in[:, :, :], x[bass.ds(b, 1)].rearrange("o (k p) d -> p (o k) d", p=P)).then_inc(S(x_loaded), 16)
                sp.dma_start(modA[:, :, :].rearrange("p m d -> p (m d)"),
                             mods_dram[bass.ds(b, 1), SA * D:(CA + 1) * D].broadcast_to([P, 2 * D])).then_inc(S(modA_loaded), 16)

            sp.wait_ge(su_dve, SU_LINKS)
            sp.dma_start(mods_dram, mods[:, :, :].rearrange("b m d -> b (m d)")).then_inc(mods_stored, 16)
            sp.wait_ge(mods_stored, 16)
            load_next(0)

            def body(i, attn, ffn, first):
                if attn:
                    if ffn:
                        sp.wait_ge(S(x2_ready), at(x2_ready, i - 1, 1))
                        sp.wait_ge(S(h2_ready), at(h2_ready, i - 1, 1))
                    sp.dma_start(x_res[:, :, :], x[bass.ds(i, 1)].rearrange("o (k p) d -> p (o k) d", p=P)).then_inc(S(res_loaded), 16)
                    sp.dma_start(modB[:, :, :].rearrange("p m d -> p (m d)"),
                                 mods_dram[bass.ds(i, 1), SB * D:(GA + 1) * D].broadcast_to([P, 3 * D])).then_inc(S(modB_loaded), 16)
                    if not (isinstance(i, int) and i + 1 >= B):
                        sp.wait_ge(S(xr_ready), at(xr_ready, i, 1))
                        load_next(i + 1)
                if ffn:
                    sp.wait_ge(S(yo_ready), at(yo_ready, i - 1, 1))
                    sp.dma_start(out[bass.ds(i - 1, 1)].rearrange("o (k p) d -> p (o k) d", p=P), yo[:, :, :]).then_inc(S(out_stored), 16)
                if attn:
                    sp.dma_start(modC[:, :, :].rearrange("p m d -> p (m d)"),
                                 mods_dram[bass.ds(i, 1), GB * D:(GD + 1) * D].broadcast_to([P, 2 * D])).then_inc(S(modC_loaded), 16)

            run(sp, body)
            sp.wait_ge(S(out_stored), at(out_stored, B, 0))

        @block.gpsimd
        def _(pool):
            nc.gpsimd.memset(ident[:, :], 0.0)
            nc.gpsimd.memset(ident_bf[:, :], 0.0)
            nc.gpsimd.memset(mask[:, :], 0.0)
            nc.gpsimd.memset(expo[:, :], -0.5)
            nc.gpsimd.memset(v[:, :, :, DH:DH + 1], 1.0).then_inc(const_pool, 1)
            pool.wait_ge(const_pool, 1)
            nc.gpsimd.affine_select(out=ident[:, :], in_=ident[:, :], compare_op=ALU.not_equal, fill=1.0,
                                    base=0, pattern=[[-1, P]], channel_multiplier=1)
            nc.gpsimd.affine_select(out=ident_bf[:, :], in_=ident_bf[:, :], compare_op=ALU.not_equal, fill=1.0,
                                    base=0, pattern=[[-1, P]], channel_multiplier=1)
            nc.gpsimd.affine_select(out=mask[:, :], in_=mask[:, :], compare_op=ALU.is_ge, fill=MASKED,
                                    base=0, pattern=[[-1, P]], channel_multiplier=1).then_inc(const_pool, 1)

            def apart():
                pool.nop(nofuse=True)

            def rstd1(b):
                pool.wait_ge(S(rstd1_in), at(rstd1_in, b, 1))
                apart()
                nc.gpsimd.tensor_scalar(ve1[:, :], mv1[:, :, 1], LN_EPS, None, ALU.add).then_inc(S(pool_chain1), 1)
                pool.wait_ge(S(pool_chain1), at(pool_chain1, b, 1))
                nc.gpsimd.tensor_tensor(rs1[:, :], ve1[:, :], expo[:, :], ALU.pow).then_inc(S(rstd1_out), 1)
                pool.wait_ge(S(rstd1_in), at(rstd1_in, b, 2))
                apart()
                nc.gpsimd.tensor_scalar(me1[:, :], ms1[:, :], 1.0 / D, RMS_EPS, ALU.mult, ALU.add).then_inc(S(pool_chain1), 1)
                pool.wait_ge(S(pool_chain1), at(pool_chain1, b, 2))
                nc.gpsimd.tensor_tensor(rr1[:, :], me1[:, :], expo[:, :], ALU.pow).then_inc(S(rstd1_out), 1)

            rstd1(0)

            def body(i, attn, ffn, first):
                f = i - 1
                if ffn:
                    pool.wait_ge(S(rstd2_in), at(rstd2_in, f, 1))
                    apart()
                    nc.gpsimd.tensor_scalar(ve2[:, :], mv2[:, :, 1], LN_EPS, None, ALU.add).then_inc(S(pool_chain2), 1)
                    pool.wait_ge(S(pool_chain2), at(pool_chain2, f, 1))
                    nc.gpsimd.tensor_tensor(rs2[:, :], ve2[:, :], expo[:, :], ALU.pow).then_inc(S(rstd2_out), 1)
                    pool.wait_ge(S(x2_ready), at(x2_ready, f, 1))
                    pool.wait_ge(S(modC_loaded), at(modC_loaded, f, 16))
                    nc.gpsimd.tensor_tensor(x2g[:, :, :], x2[:, :, :], modC[:, 1:2, :].broadcast_to([P, TB, D]),
                                            ALU.add).then_inc(S(x2g_ready), 1)
                if attn and not (isinstance(i, int) and i + 1 >= B):
                    rstd1(i + 1)
                if ffn:
                    pool.wait_ge(S(xs_ready), at(xs_ready, f, 1))
                    for k in range(TB):
                        for h in range(RH):
                            ins = nc.gpsimd.tensor_tensor(
                                fsum[:, k, h], xs[:, k, h, :].unsqueeze(2).broadcast_to([P, NX, NK]),
                                ys[:, k, h, :].unsqueeze(1).broadcast_to([P, NX, NK]), ALU.add)
                        ins.then_inc(S(f_ready), 1)
                    pool.wait_ge(S(fexp_ready), at(fexp_ready, f, 1))
                    pool.wait_ge(S(masks_ready), at(masks_ready, f, 1))
                    nc.gpsimd.tensor_tensor(fexp[:, 0], fexp[:, 0], chosen[:, :, :], ALU.mult).then_inc(S(pool_sum), 1)
                    pool.wait_ge(S(pool_sum), at(pool_sum, f, 1))
                    nc.gpsimd.tensor_tensor(ws2[:, :, :], fexp[:, 0, 0:2, :], fexp[:, 0, 2:4, :], ALU.add).then_inc(S(pool_sum), 1)
                    pool.wait_ge(S(pool_sum), at(pool_sum, f, 2))
                    nc.gpsimd.tensor_tensor(wsum[:, 0, :], ws2[:, 0, :], ws2[:, 1, :], ALU.add).then_inc(S(pool_sum), 1)
                    pool.wait_ge(S(wsum_ready), at(wsum_ready, f, 1))
                    e = work_free[bank_of["D", 1], "f"]
                    pool.wait_ge(S(e), at(e, f, place["D", 1] + 1))
                    nc.gpsimd.tensor_tensor(eo[:, 1, :], d_s[:, 1, :], wsum[:, 1, :], ALU.mult).then_inc(S(eo_ready), 1)
                    pool.wait_ge(S(tot_ready), at(tot_ready, f, 1))
                    apart()
                    nc.gpsimd.tensor_scalar(tot[:, 0:1], tot[:, 0:1], -1.0, float(RH), ALU.mult, ALU.add).then_inc(S(pool_sum), 1)
                    pool.wait_ge(S(pool_sum), at(pool_sum, f, 4))
                    nc.gpsimd.tensor_tensor(wsum[:, 0, NE - 1:NE], wsum[:, 0, NE - 1:NE], tot[:, 0:1], ALU.add).then_inc(S(pool_sum), 1)
                    pool.wait_ge(S(pool_sum), at(pool_sum, f, 5))
                    nc.gpsimd.tensor_tensor(eo[:, 0, :], d_s[:, 0, :], wsum[:, 0, :], ALU.mult).then_inc(S(eo_ready), 1)

            run(pool, body)

        @block.scalar
        def _(act):
            act.dma_start(c_sb[:, :], cond).then_inc(load_c, 16)
            act.dma_start(wmod_sb[:, :], wmod).then_inc(load_c, 16)
            act.dma_start(bd_sb[:, :], fbd.rearrange("(o d) -> o d", o=1).broadcast_to([B, D])).then_inc(load_c, 16)
            for a in range(2):
                act.dma_start(fwq_sb[:, :, a, :], fWq[:, a * RH * KD:(a + 1) * RH * KD].rearrange("d (h n) -> d h n", h=RH)).then_inc(load_c, 16)
            act.dma_start(key_sb[:, :, :], keys.rearrange("h k p n -> k h (p n)")).then_inc(load_c, 16)
            act.dma_start(down_sb[:, :, :], down.rearrange("(c p) d -> p c d", p=P)).then_inc(load_c, 16)
            act.wait_ge(load_c, 112)
            nc.scalar.activation(c_th[:, :], c_sb[:, :], ACT.Tanh, scale=0.5).then_inc(su_act, 1)

            def body(i, attn, ffn, first):
                w = Work(act, i, attn, ffn)
                w.first_loop = first
                f = i - 1

                def evacuate(dst, src, name, k=0):
                    w.wait_full(name, k)
                    w.release(nc.scalar.copy(dst, src), name, k)

                if attn:
                    evacuate(xT[:, :], w.bank("xT")[:, 0:N], "xT")
                    for p in range(2):
                        evacuate(qk[:, p, :], w.bank("QK", p)[:, :], "QK", p)

                def values(n):
                    k, half = divmod(n, 2)
                    evacuate(v[:, k, half * 8:half * 8 + 8, 0:DH],
                             w.bank("V", n)[:, :].rearrange("p (h d) -> p h d", h=8), "V", n)

                if attn:
                    for n in range(TB):
                        values(n)
                for s in range(NSTEP):
                    if ffn:
                        if s == 1:
                            evacuate(h2T[:, :], w.bank("hT")[:, 0:N], "hT")
                        if s in (2, 3):
                            k = s - 2
                            w.wait_full("D", k)
                            nc.scalar.activation(d_t[:, k, :], w.bank("D", k)[:, :], ACT.Tanh, scale=0.5).then_inc(S(d_act), 1)
                        if 3 <= s < 3 + FC:
                            c = s - 3
                            w.wait_full("GU", c)
                            bank = w.bank("GU", c)
                            nc.scalar.activation(g_t[:, c, :], bank[:, 0:N], ACT.Tanh, bias=b_gh[:, c:c + 1], scale=0.5)
                            nc.scalar.activation(u_sb[:, c, :], bank[:, N:2 * N], ACT.Identity,
                                                 bias=b_u[:, c:c + 1]).then_inc(S(gu_act), 1)
                        if s in (8, 9):
                            k = ET_BLOCK[s - 8]
                            evacuate(eT[:, k].rearrange("p c t -> p (c t)"), w.bank("ET", s - 8)[:, :], "ET", s - 8)
                    if attn and s == 0:
                        for n in range(TB, 2 * TB):
                            values(n)
                    if attn and s + 2 < NP:
                        if s + 2 >= 4:
                            act.wait_ge(S(s_full), at(s_full, i, s - 1))
                        evacuate(qk[:, (s + 2) % 4, :], w.bank("QK", s + 2)[:, :], "QK", s + 2)
                    if attn and s == 0:
                        w.wait_full("gate")
                        w.release(nc.scalar.activation(g_th[:, :, :].rearrange("p k h -> p (k h)"), w.bank("gate")[:, 0:TB * H],
                                                       ACT.Tanh, scale=0.5), "gate")
                    if attn and 2 <= s:
                        evacuate(aoT[:, s - 2, :], w.bank("AO", s - 2)[:, 0:N], "AO", s - 2)
                    if ffn and s == 1:
                        for k in range(TB):
                            evacuate(sim[:, k].rearrange("p a h n -> p (a h n)"), w.bank("sim", k)[:, :], "sim", k)
                    if attn and s < NP:
                        act.wait_ge(S(t_full), at(t_full, i, s + 1))
                        if s >= 2:
                            w.wait_full("PV", s - 2)
                        nc.scalar.activation(pT[:, s % 2], pTT[:, :, 0:SW], ACT.Exp, scale=SCALE).then_inc(S(exp_done), 1)
                    if ffn:
                        if s == 3:
                            act.wait_ge(S(top_ready), at(top_ready, f, 1))
                            nc.scalar.activation(e8[:, :, :, :], top8[:, :, :, :], ACT.Exp).then_inc(S(e8_ready), 1)
                        if s in (3, 4):
                            k = s - 3
                            act.wait_ge(S(f_ready), at(f_ready, f, k + 1))
                            nc.scalar.activation(fexp[:, k].rearrange("p h e -> p (h e)"),
                                                 fsum[:, k].rearrange("p h i j -> p (h i j)"), ACT.Exp).then_inc(S(fexp_ready), 1)
                        if s == 7:
                            act.wait_ge(S(pool_sum), at(pool_sum, f, 3))
                            nc.scalar.activation(junk[:, :], wsum[:, 0, :], ACT.Copy, accum_out=tot[:, 0:1]).then_inc(S(tot_ready), 1)

            act.wait_ge(su_pe, 2)
            nc.scalar.copy(fwqT[:, :], pS[:, 0, :]).then_inc(su_act, 1)
            act.wait_ge(su_pe, 3)
            nc.scalar.copy(keyT[:, :], pS[:, 1, 0:RH * NK]).then_inc(su_act, 1)
            act.wait_ge(su_pe, 4)
            nc.scalar.copy(w_down[:, :], pW[2][:, :]).then_inc(su_act, 1)
            act.wait_ge(su_pe, 5)
            nc.scalar.copy(w_sim[:, 0:RH * NK], pTT[:, 0, 0:RH * NK])
            nc.scalar.copy(w_sim[:, RH * NK:2 * RH * NK], pTT[:, 1, 0:RH * NK]).then_inc(su_act, 1)
            run(act, body)

        @block.vector
        def _(dve):
            n_links = {ln1_chain: 0, attn_chain: 0, ffn_chain: 0}

            def link(ins, chain, b):
                n_links[chain] += 1
                ins.then_inc(S(chain), 1)
                dve.wait_ge(S(chain), at(chain, b, n_links[chain]))

            def apart():
                dve.nop(nofuse=True)

            def done(chain):
                assert n_links[chain] == per[chain][1], (chain, n_links[chain])
                n_links[chain] = 0

            su = [0]

            def su_link(ins):
                su[0] += 1
                ins.then_inc(su_dve, 1)
                dve.wait_ge(su_dve, su[0])

            dve.wait_ge(load_c, 112)
            dve.wait_ge(su_act, 1)
            su_link(nc.vector.scalar_tensor_tensor(out=c_silu[:, :], in0=c_th[:, :], scalar=1.0, in1=c_sb[:, :], op0=ALU.add, op1=ALU.mult))
            su_link(nc.vector.tensor_scalar(c_silu[:, :], c_silu[:, :], 0.5, None, ALU.mult))
            dve.wait_ge(su_pe, 1)
            su_link(nc.vector.tensor_copy(cT[:, :], pW[0][:, 0:B]))
            dve.wait_ge(load_qkv, 64)
            nc.vector.tensor_scalar(w_qkv[:, :], w_qkv[:, :], nw[:, 0:1], None, ALU.mult)
            nc.vector.tensor_scalar(w_gate[:, :], w_gate[:, :], nw[:, 0:1], None, ALU.mult)
            dve.wait_ge(load_w, 112)
            nc.vector.tensor_scalar(w_out[:, :, :], w_out[:, :, :], 0.5, None, ALU.mult)
            nc.vector.tensor_scalar(w_d[:, :, :], w_d[:, :, :], 0.5, None, ALU.mult)
            nc.vector.tensor_scalar(w_up[:, :, :], w_up[:, :, :], 0.5, None, ALU.mult)
            nc.vector.tensor_scalar(b_gh[:, :], b_g[:, :], 0.5, None, ALU.mult).then_inc(const_dve, 1)
            dve.wait_ge(su_pe, 6)
            nc.vector.tensor_copy(mod_sb[:, 0:BANK], pW[0][0:B, :])
            su_link(nc.vector.tensor_copy(mod_sb[:, BANK:6 * D], pW[1][0:B, 0:6 * D - BANK]))
            m6 = mod_sb[:, :].rearrange("b (m d) -> b m d", m=6)
            gates = m6[:, 2:6:3, :]
            nc.vector.tensor_copy(mods[:, SA, :], m6[:, 0, :])
            nc.vector.tensor_scalar(mods[:, CA, :], m6[:, 1, :], 1.0, None, ALU.add)
            nc.vector.tensor_copy(mods[:, SB, :], m6[:, 3, :])
            nc.vector.tensor_scalar(mods[:, CB, :], m6[:, 4, :], 1.0, None, ALU.add)
            nc.vector.tensor_scalar(sgn[:, :, :], gates, 0.0, 2.0, ALU.is_ge, ALU.mult)
            su_link(nc.vector.scalar_tensor_tensor(out=mag[:, :, :], in0=gates, scalar=-1.0, in1=gates, op0=ALU.mult, op1=ALU.max))
            su_link(nc.vector.tensor_scalar(sgn[:, :, :], sgn[:, :, :], -1.0, None, ALU.add))
            su_link(nc.vector.scalar_tensor_tensor(out=mods[:, GA:GB + 1, :], in0=mag[:, :, :], scalar=0.25, in1=sgn[:, :, :],
                                                   op0=ALU.max, op1=ALU.mult))
            su_link(nc.vector.tensor_tensor(mods[:, GD, :], mods[:, GB, :], bd_sb[:, :], ALU.mult))

            def ln1_stats(b):
                dve.wait_ge(S(x_loaded), at(x_loaded, b, 16))
                for k in range(TB):
                    ins = nc.vector.bn_stats(st1[:, k, :], x_in[:, k, :])
                link(ins, ln1_chain, b)
                apart()
                for k in range(TB):
                    ins = nc.vector.bn_aggr(mv1[:, k, :], st1[:, k, :])
                ins.then_inc(S(rstd1_in), 1)

            def ln1_modulate(b):
                dve.wait_ge(S(rstd1_out), at(rstd1_out, b, 1))
                dve.wait_ge(S(modA_loaded), at(modA_loaded, b, 16))
                for k in range(TB):
                    ins = nc.vector.tensor_scalar(h1[:, k, :], x_in[:, k, :], mv1[:, k, 0:1], rs1[:, k:k + 1], ALU.subtract, ALU.mult)
                link(ins, ln1_chain, b)
                link(nc.vector.tensor_tensor(h1[:, :, :], h1[:, :, :], modA[:, 1:2, :].broadcast_to([P, TB, D]), ALU.mult), ln1_chain, b)
                link(nc.vector.tensor_tensor(h1[:, :, :], h1[:, :, :], modA[:, 0:1, :].broadcast_to([P, TB, D]), ALU.add), ln1_chain, b)
                for k in range(TB):
                    ins = nc.vector.tensor_tensor_reduce(out=sq1[:, k, :], in0=h1[:, k, :], in1=h1[:, k, :], scale=1.0, scalar=0.0,
                                                         op0=ALU.mult, op1=ALU.add, accum_out=ms1[:, k:k + 1])
                ins.then_inc(S(rstd1_in), 1)

            def ln1_rms(b):
                dve.wait_ge(S(rstd1_out), at(rstd1_out, b, 2))
                for k in range(TB):
                    ins = nc.vector.tensor_scalar(xr[:, k, :], h1[:, k, :], rr1[:, k:k + 1], None, ALU.mult)
                ins.then_inc(S(xr_ready), 1)
                done(ln1_chain)

            ln1_stats(0)
            ln1_modulate(0)
            ln1_rms(0)

            def body(i, attn, ffn, first):
                w = Work(dve, i, attn, ffn)
                w.first_loop = first
                f = i - 1
                ahead = attn and not (isinstance(i, int) and i + 1 >= B)
                if ffn:
                    dve.wait_ge(S(res_loaded), at(res_loaded, f, 16))
                    dve.wait_ge(S(modB_loaded), at(modB_loaded, f, 16))
                    for k in range(TB):
                        w.wait_full("op", k)
                        ins = nc.vector.tensor_tensor(ga_o[:, k, :], w.bank("op", k)[:, 0:D], modB[:, 2, :], ALU.mult)
                        w.release(ins, "op", k)
                    e = work_free[w.key("op", TB - 1)]
                    dve.wait_ge(S(e), at(e, f, place["op", TB - 1] + 1))
                    ins = nc.vector.tensor_tensor(x2[:, :, :], ga_o[:, :, :], x_res[:, :, :], ALU.add)
                    ins.then_inc(S(x2_ready), 1)
                    dve.wait_ge(S(x2_ready), at(x2_ready, f, 1))
                    for k in range(TB):
                        ins = nc.vector.bn_stats(st2[:, k, :], x2[:, k, :])
                    link(ins, ffn_chain, f)
                    apart()
                    for k in range(TB):
                        ins = nc.vector.bn_aggr(mv2[:, k, :], st2[:, k, :])
                    ins.then_inc(S(rstd2_in), 1)
                for s in range(NSTEP):
                    if attn and s < NP:
                        slot = s % 2
                        dve.wait_ge(S(s_full), at(s_full, i, s + 1))
                        nc.vector.reduce_max(mx[:, slot, :, 0], pS[:, :, 0:P], AX_X)
                        link(nc.vector.reduce_max(mx[:, slot, :, 1], pS[:, :, P:SW], AX_X), attn_chain, i)
                        if s >= 2:
                            dve.wait_ge(S(t_full), at(t_full, i, s - 1))
                        nc.vector.tensor_tensor(s_sb[:, slot, :, 0:P], pS[:, :, 0:P],
                                                mx[:, slot, :, 0:1].broadcast_to([P, 2, P]), ALU.subtract)
                        nc.vector.tensor_tensor(s_sb[:, slot, :, P:SW], pS[:, :, P:SW],
                                                mx[:, slot, :, 1:2].broadcast_to([P, 2, SW - P]), ALU.subtract).then_inc(S(s_taken), 1)
                    if attn and 1 <= s < NP + 1:
                        p = s - 1
                        if p == 0:
                            e = work_free[w.key("gate", 0)]
                            dve.wait_ge(S(e), at(e, i, place["gate", 0] + 1))
                        w.wait_full("PV", p)
                        pv = w.bank("PV", p)[:, 0:2 * TB * (DH + 1)].rearrange("p (h k e) -> p h k e", h=2, k=TB)
                        link(nc.vector.reciprocal(rden[:, :, :], pv[:, :, :, DH]), attn_chain, i)
                        link(nc.vector.scalar_tensor_tensor(out=coef[:, :, :], in0=g_th[:, :, 2 * p:2 * p + 2].rearrange("p k h -> p h k"),
                                                            scalar=1.0, in1=rden[:, :, :], op0=ALU.add, op1=ALU.mult), attn_chain, i)
                        if p >= 2:
                            e = work_full[w.key("AO", p - 2)]
                            dve.wait_ge(S(e), at(e, i, place["AO", p - 2] + 1))
                        ins = nc.vector.tensor_tensor(ao[:, p % 2].rearrange("p k (h d) -> p h k d", h=2), pv[:, :, :, 0:DH],
                                                      coef[:, :, :].unsqueeze(3).broadcast_to([P, 2, TB, DH]), ALU.mult)
                        w.release(ins, "PV", p)
                    if ffn:
                        if s == 0:
                            dve.wait_ge(S(rstd2_out), at(rstd2_out, f, 1))
                            for k in range(TB):
                                ins = nc.vector.tensor_scalar(h2[:, k, :], x2[:, k, :], mv2[:, k, 0:1], rs2[:, k:k + 1], ALU.subtract, ALU.mult)
                            link(ins, ffn_chain, f)
                            link(nc.vector.tensor_tensor(h2[:, :, :], h2[:, :, :], modB[:, 1:2, :].broadcast_to([P, TB, D]), ALU.mult), ffn_chain, f)
                            nc.vector.tensor_tensor(h2[:, :, :], h2[:, :, :], modB[:, 0:1, :].broadcast_to([P, TB, D]), ALU.add).then_inc(S(h2_ready), 1)
                        if s in (2, 3):
                            k = s - 2
                            dve.wait_ge(S(d_act), at(d_act, f, k + 1))
                            ins = nc.vector.scalar_tensor_tensor(out=d_s[:, k, :], in0=d_t[:, k, :], scalar=1.0, in1=w.bank("D", k)[:, :],
                                                                 op0=ALU.add, op1=ALU.mult)
                            w.release(ins, "D", k)
                        if 3 <= s < 3 + FC:
                            c = s - 3
                            dve.wait_ge(S(gu_act), at(gu_act, f, c + 1))
                            w.release(nc.vector.scalar_tensor_tensor(out=gu[:, c, :], in0=w.bank("GU", c)[:, 0:N], scalar=b_g[:, c:c + 1],
                                                                     in1=u_sb[:, c, :], op0=ALU.add, op1=ALU.mult), "GU", c)
                        if s == 2:
                            for k in range(TB):
                                e = work_free[w.key("sim", k)]
                                dve.wait_ge(S(e), at(e, f, place["sim", k] + 1))
                                apart()
                                for a in range(2):
                                    for h in range(RH):
                                        ins = nc.vector.max(tops[:, a, k, h, :], sim[:, k, a, h, :])
                            link(ins, ffn_chain, f)
                            nc.vector.tensor_tensor(xs[:, :, :, :], sim[:, :, 0, :, 0:NX], tops[:, 0, :, :, 0:1].broadcast_to([P, TB, RH, NX]),
                                                    ALU.subtract)
                            nc.vector.tensor_tensor(ys[:, :, :, :], sim[:, :, 1, :, :], tops[:, 1, :, :, 0:1].broadcast_to([P, TB, RH, NK]),
                                                    ALU.subtract).then_inc(S(xs_ready), 1)
                        if s == 3:
                            link(nc.vector.tensor_tensor(sxy[:, :, :, :, :].rearrange("p a k h t -> p (a k h) t"),
                                                         tops[:, :, :, :, :].rearrange("p a k h t -> p (a k h) t"),
                                                         tops[:, :, :, :, 0:1].rearrange("p a k h t -> p (a k h) t").broadcast_to([P, 2 * TB * RH, TK]),
                                                         ALU.subtract), ffn_chain, f)
                            link(nc.vector.tensor_tensor(
                                cand[:, :, :, :, :].rearrange("p k h a b -> p (k h) a b"),
                                sxy[:, 0].rearrange("p k h a -> p (k h) a").unsqueeze(3).broadcast_to([P, TB * RH, TK, TK]),
                                sxy[:, 1].rearrange("p k h a -> p (k h) a").unsqueeze(2).broadcast_to([P, TB * RH, TK, TK]),
                                ALU.add), ffn_chain, f)
                            apart()
                            for kk in range(TB):
                                for h in range(RH):
                                    ins = nc.vector.max(top8[:, kk, h, :], cand[:, kk, h].rearrange("p a b -> p (a b)"))
                            ins.then_inc(S(top_ready), 1)
                        if s == 4:
                            dve.wait_ge(S(e8_ready), at(e8_ready, f, 1))
                            link(nc.vector.reduce_sum(zz[:, :, :], e8[:, :, :, :], AX_X), ffn_chain, f)
                            link(nc.vector.reciprocal(rz[:, :, :], zz[:, :, :]), ffn_chain, f)
                            dve.wait_ge(S(f_ready), at(f_ready, f, 1))
                            for h in range(RH):
                                ins = nc.vector.tensor_scalar(chosen[:, h, :], fsum[:, 0, h].rearrange("p i j -> p (i j)"),
                                                              top8[:, 0, h, TK - 1:TK], rz[:, 0, h:h + 1], ALU.is_ge, ALU.mult)
                            ins.then_inc(S(masks_ready), 1)
                        if s == 5:
                            dve.wait_ge(S(fexp_ready), at(fexp_ready, f, 2))
                            for h in range(RH):
                                ins = nc.vector.scalar_tensor_tensor(
                                    out=fexp[:, 1, h, :], in0=fsum[:, 1, h].rearrange("p i j -> p (i j)"), scalar=top8[:, 1, h, TK - 1:TK],
                                    in1=fexp[:, 1, h, :], op0=ALU.is_ge, op1=ALU.mult)
                            link(ins, ffn_chain, f)
                        if s == 6:
                            link(nc.vector.tensor_scalar(wsum[:, 1, :], fexp[:, 1, 0, :], rz[:, 1, 0:1], None, ALU.mult), ffn_chain, f)
                            for h in range(1, RH):
                                link(nc.vector.scalar_tensor_tensor(out=wsum[:, 1, :], in0=fexp[:, 1, h, :], scalar=rz[:, 1, h:h + 1],
                                                                    in1=wsum[:, 1, :], op0=ALU.mult, op1=ALU.add,
                                                                    accum_out=tot[:, 1:2] if h == RH - 1 else None), ffn_chain, f)
                            link(nc.vector.tensor_scalar(tot[:, 1:2], tot[:, 1:2], -1.0, float(RH), ALU.mult, ALU.add), ffn_chain, f)
                            nc.vector.tensor_tensor(wsum[:, 1, NE - 1:NE], wsum[:, 1, NE - 1:NE], tot[:, 1:2],
                                                    ALU.add).then_inc(S(wsum_ready), 1)
                        if s == 7:
                            e = work_free[w.key("GU", FC - 1)]
                            dve.wait_ge(S(e), at(e, f, place["GU", FC - 1] + 1))
                            nc.vector.scalar_tensor_tensor(out=m_sb[:, :, :].rearrange("p c t -> p (c t)"), in0=g_t[:, :, :].rearrange("p c t -> p (c t)"),
                                                           scalar=1.0, in1=gu[:, :, :].rearrange("p c t -> p (c t)"),
                                                           op0=ALU.add, op1=ALU.mult).then_inc(S(gu_ready), 1)
                    if ahead:
                        if s == 0:
                            ln1_stats(i + 1)
                        if s == 1:
                            ln1_modulate(i + 1)
                        if s == 2:
                            ln1_rms(i + 1)
                if ffn:
                    w.wait_full("y")
                    dve.wait_ge(S(modC_loaded), at(modC_loaded, f, 16))
                    ins = nc.vector.tensor_tensor(y_g[:, :, :], w.bank("y")[:, 0:N].rearrange("p (k d) -> p k d", k=TB),
                                                  modC[:, 0:1, :].broadcast_to([P, TB, D]), ALU.mult)
                    w.release(ins, "y")
                    e = work_free[w.key("y", 0)]
                    dve.wait_ge(S(e), at(e, f, place["y", 0] + 1))
                    dve.wait_ge(S(x2g_ready), at(x2g_ready, f, 1))
                    if not first:
                        dve.wait_ge(S(out_stored), at(out_stored, f, 0))
                    nc.vector.tensor_tensor(yo[:, :, :], y_g[:, :, :], x2g[:, :, :], ALU.add).then_inc(S(yo_ready), 1)
                    done(ffn_chain)
                if attn:
                    done(attn_chain)

            run(dve, body)

        @block.tensor
        def _(pe):
            mm, tp = nc.tensor.matmul, nc.tensor.transpose
            pe.wait_ge(const_pool, 2)
            pe.wait_ge(su_dve, 2)
            tp(pW[0][:, 0:B], c_silu[:, :], ident[0:B, 0:B]).then_inc(su_pe, 1)
            pe.wait_ge(load_c, 112)
            for h in range(RH):
                ins = tp(pS[:, 0, h * D:(h + 1) * D], fwq_sb[:, h].rearrange("d p n -> d (p n)"), ident[:, :])
            ins.then_inc(su_pe, 1)
            for h in range(RH):
                ins = tp(pS[:, 1, h * NK:(h + 1) * NK], key_sb[:, h, :], ident[0:NK, 0:NK])
            ins.then_inc(su_pe, 1)
            for c in range(EC):
                ins = tp(pW[2][:, c * P:(c + 1) * P], down_sb[:, c, :], ident[:, :])
            ins.then_inc(su_pe, 1)
            pe.wait_ge(su_act, 3)
            for a in range(2):
                rows = slice(a * KD, (a + 1) * KD)
                for h in range(RH):
                    ins = mm(pTT[:, a, h * NK:(h + 1) * NK], fwqT[rows, h * D:(h + 1) * D], keyT[rows, h * NK:(h + 1) * NK],
                             start=True, stop=True)
            ins.then_inc(su_pe, 1)
            pe.wait_ge(su_dve, 3)
            mm(pW[0][0:B, :], cT[:, :], wmod_sb[:, 0:BANK], start=True, stop=True)
            mm(pW[1][0:B, 0:6 * D - BANK], cT[:, :], wmod_sb[:, BANK:6 * D], start=True, stop=True).then_inc(su_pe, 1)
            pe.wait_ge(su_act, 5)
            pe.wait_ge(su_dve, 4)
            pe.wait_ge(const_dve, 1)

            def body(i, attn, ffn, first):
                w = Work(pe, i, attn, ffn)
                w.first_loop = first
                f = i - 1

                def released(name, k=0):
                    e = work_free[w.key(name, k)]
                    pe.wait_ge(S(e), at(e, w.batch(name, k), place[name, k] + 1))

                def project_qk(p):
                    w.wait_free("QK", p)
                    bank = w.bank("QK", p)
                    mm(bank[:, 0:N], w_qkv[:, p * P:(p + 1) * P], xT[:, :], start=True, stop=True)
                    w.filled(mm(bank[:, N:2 * N], w_qkv[:, DI + p * P:DI + (p + 1) * P], xT[:, :], start=True, stop=True), "QK", p)

                def project_v(n):
                    k, half = divmod(n, 2)
                    w.wait_free("V", n)
                    w.filled(mm(w.bank("V", n)[:, :], xT[:, k * P:(k + 1) * P], w_qkv[:, 2 * DI + half * BANK:2 * DI + (half + 1) * BANK],
                                start=True, stop=True), "V", n)

                def scores(p):
                    released("QK", p)
                    if p >= 1 or not (isinstance(i, int) and i == 0):
                        pe.wait_ge(S(s_taken), at(s_taken, i, p))
                    ps = pS
                    for h in range(2):
                        r = slice(h * DH, (h + 1) * DH)
                        mm(ps[:, h, 0:P], qk[r, p % 4, 0:P], qk[r, p % 4, N:N + P], start=True, stop=False, skip_group_check=True)
                    for h in range(2):
                        r = slice(h * DH, (h + 1) * DH)
                        mm(ps[:, h, P:SW], qk[r, p % 4, P:N], qk[r, p % 4, N:2 * N], start=False, stop=False, skip_group_check=True)
                    for h in range(2):
                        mm(ps[:, h, 0:P], ident_bf[:, :], mask[:, :], start=False, stop=True, skip_group_check=True)
                        ins = mm(ps[:, h, 2 * P:SW], ident_bf[:, :], mask[:, :], start=False, stop=True, skip_group_check=True)
                    ins.then_inc(S(s_full), 1)

                def transpose_scores(p):
                    pe.wait_ge(S(s_taken), at(s_taken, i, p + 1))
                    if p >= 1:
                        pe.wait_ge(S(exp_done), at(exp_done, i, p))
                    elif not (isinstance(i, int) and i == 0):
                        pe.wait_ge(S(exp_done), at(exp_done, i, 0))
                    for h in range(2):
                        for b in range(BLOCKS):
                            ins = tp(pTT[:, h, b * P:(b + 1) * P], s_sb[:, p % 2, h, b * P:(b + 1) * P], ident[:, :])
                    ins.then_inc(S(t_full), 1)

                def weigh_values(p):
                    if p == 0:
                        released("V", 2 * TB - 1)
                    pe.wait_ge(S(exp_done), at(exp_done, i, p + 1))
                    w.wait_free("PV", p)
                    bank = w.bank("PV", p)
                    E1 = DH + 1
                    for h in range(2):
                        hh = 2 * p + h
                        o0, o1 = (2 * h) * E1, (2 * h + 1) * E1
                        mm(bank[:, o0:o0 + E1], pT[:, p % 2, h, 0:P], v[:, 0, hh, :], start=True, stop=True)
                        mm(bank[:, o1:o1 + E1], pT[:, p % 2, h, P:2 * P], v[:, 0, hh, :], start=True, stop=False)
                        ins = mm(bank[:, o1:o1 + E1], pT[:, p % 2, h, 2 * P:3 * P], v[:, 1, hh, :], start=False, stop=True)
                    w.filled(ins, "PV", p)

                def project_gate():
                    w.wait_free("gate")
                    for k in range(TB):
                        ins = mm(w.bank("gate")[:, k * H:(k + 1) * H], xT[:, k * P:(k + 1) * P], w_gate[:, :], start=True, stop=True)
                    w.filled(ins, "gate")

                def transpose_out(p):
                    released("PV", p)
                    w.wait_free("AO", p)
                    for k in range(TB):
                        ins = tp(w.bank("AO", p)[:, k * P:(k + 1) * P], ao[:, p % 2, k, :], ident[:, :])
                    w.filled(ins, "AO", p)

                def second_half(step):
                    if step == 1:
                        pe.wait_ge(S(h2_ready), at(h2_ready, f, 1))
                        w.wait_free("hT")
                        for k in range(TB):
                            ins = tp(w.bank("hT")[:, k * P:(k + 1) * P], h2[:, k, :], ident[:, :])
                        w.filled(ins, "hT")
                    if step in (2, 3):
                        k = step - 2
                        w.wait_free("D", k)
                        w.filled(mm(w.bank("D", k)[:, :], h2T[:, k * P:(k + 1) * P], w_down[:, :], start=True, stop=True), "D", k)
                    if 3 <= step < 3 + FC:
                        c = step - 3
                        w.wait_free("GU", c)
                        bank = w.bank("GU", c)
                        mm(bank[:, 0:N], w_g[:, c * P:(c + 1) * P], h2T[:, :], start=True, stop=True)
                        w.filled(mm(bank[:, N:2 * N], w_u[:, c * P:(c + 1) * P], h2T[:, :], start=True, stop=True), "GU", c)
                    if step in (8, 9):
                        n = step - 8
                        pe.wait_ge(S(eo_ready), at(eo_ready, f, n + 1))
                        w.wait_free("ET", n)
                        for c in range(EC):
                            ins = tp(w.bank("ET", n)[:, c * P:(c + 1) * P], eo[:, ET_BLOCK[n], c * P:(c + 1) * P], ident[:, :])
                        w.filled(ins, "ET", n)
                    if step == NSTEP - 1:
                        pe.wait_ge(S(gu_ready), at(gu_ready, f, 1))
                        w.wait_free("y")
                        for k in ET_BLOCK:
                            o = w.bank("y")[:, k * D:(k + 1) * D]
                            for c in range(FC):
                                mm(o, m_sb[:, c, k * P:(k + 1) * P], w_d[:, c, :], start=c == 0, stop=False)
                            released("ET", ET_BLOCK.index(k))
                            for c in range(EC):
                                ins = mm(o, eT[:, k, c, :], w_up[:, c, :], start=False, stop=c == EC - 1)
                        w.filled(ins, "y")

                if attn:
                    pe.wait_ge(S(xr_ready), at(xr_ready, i, 1))
                    w.wait_free("xT")
                    for k in range(TB):
                        ins = tp(w.bank("xT")[:, k * P:(k + 1) * P], xr[:, k, :], ident[:, :])
                    w.filled(ins, "xT")
                if attn:
                    released("xT")
                    project_qk(0)
                    project_qk(1)
                if ffn:
                    e = work_free[bank_of["AO", NP - 1], "a"]
                    pe.wait_ge(S(e), at(e, f, place["AO", NP - 1] + 1))
                    for k in range(TB):
                        w.wait_free("op", k)
                        for p in range(NP):
                            ins = mm(w.bank("op", k)[:, 0:D], aoT[:, p, k * P:(k + 1) * P], w_out[:, p, :],
                                     start=p == 0, stop=p == NP - 1)
                        w.filled(ins, "op", k)
                if attn:
                    for n in range(TB):
                        project_v(n)
                for s in range(NSTEP):
                    if attn and s < NP:
                        scores(s)
                    if ffn:
                        second_half(s)
                    if attn and s == 0:
                        for n in range(TB, 2 * TB):
                            project_v(n)
                    if attn and s + 2 < NP:
                        project_qk(s + 2)
                    if attn and s == 0:
                        project_gate()
                    if attn and 1 <= s < NP + 1:
                        weigh_values(s - 1)
                    if attn and 2 <= s:
                        transpose_out(s - 2)
                    if ffn and s == 1:
                        released("hT")
                        for k in range(TB):
                            w.wait_free("sim", k)
                            w.filled(mm(w.bank("sim", k)[:, :], h2T[:, k * P:(k + 1) * P], w_sim[:, :], start=True, stop=True), "sim", k)
                    if attn and s < NP:
                        transpose_scores(s)

            run(pe, body)


LN1_LINKS, ATTN_LINKS, FFN_LINKS, SU_LINKS = 4, 24, 14, 8

_INS = ['L0_attn_tokens', 'L0_attn_norm_w', 'L0_attn_Wq', 'L0_attn_Wkv', 'L0_attn_Wout', 'L0_attn_Wg', 'L0_ffn_Wg',
        'L0_ffn_bg', 'L0_ffn_Wu', 'L0_ffn_bu', 'L0_ffn_Wd', 'L0_ffn_bd', 'L0_ffn_Wq', 'L0_ffn_keys', 'L0_ffn_down_embed',
        'L0_ffn_up_embed', 'L0_c', 'L0_wmod']


def kernel(**inputs):
    import numpy as _np
    import concourse.bacc as _bacc
    from concourse import mybir as _mybir
    from concourse.bass_utils import run_bass_kernel_spmd as _run

    nc = _bacc.Bacc("TRN2", target_bir_lowering=False, num_devices=1)
    arrays, args = {}, []
    for name in _INS:
        a = _np.ascontiguousarray(inputs[name])
        arrays[f"in_{name}"] = a
        args.append(nc.dram_tensor(f"in_{name}", a.shape, _mybir.dt.from_np(a.dtype), kind="ExternalInput").ap())
    out = nc.dram_tensor("out", (B, N, D), _mybir.dt.float32, kind="ExternalOutput").ap()
    program(nc, *args, out)
    r = _run(nc, [arrays], core_ids=[0])
    return r.results[0]["out"]
```

```python
import concourse.bass as bass
from concourse import mybir
from contextlib import ExitStack

F32 = mybir.dt.float32
F32R = mybir.dt.float32r
BF16 = mybir.dt.bfloat16
ALU = mybir.AluOpType
ACT = mybir.ActivationFunctionType
AX_X = mybir.AxisListType.X

B, N, D = 32, 256, 128
P = 128
TB = N // P
H, DH = 16, 64
NP = H // 2
DI = H * DH
BLOCKS = TB * (TB + 1) // 2
SW = BLOCKS * P
F = 512
FC = F // P
NE = 512
EC = NE // P
RH, NK, KD, TK = 4, 64, 64, 8
NX = NE // NK
SCALE = float(DH) ** -0.5
LN_EPS = 1e-5
RMS_EPS = 2.0 ** -23
MASKED = -1e30
NSTEP = NP + 3
NW = 4
BANK = 512
AHEAD = {"a": 0, "f": -1, "x": 1}
GU_STEPS = (4, 5, 6, 8)
MLP_STEPS = (5, 6, 7, 8)
NMOD = 7
SA, CA, SB, CB, GA, GB, GD = range(NMOD)


def program(nc, x, norm_w, Wq, Wkv, Wout, Wgate, fWg, fbg, fWu, fbu, fWd, fbd, fWq, keys,
            down, up, cond, wmod, out):
    ctx = ExitStack()
    with ctx:
        def sb(name, shape, dt=F32):
            return ctx.enter_context(nc.sbuf_tensor(name, shape, dt))

        def sem(name):
            return ctx.enter_context(nc.semaphore(name))

        ident = sb("ident", [P, P])
        ident_bf = sb("ident_bf", [P, P], BF16)
        mask = sb("mask", [P, P], BF16)
        expo = sb("expo", [P, TB])
        nw = sb("nw", [P, 1])
        w_out = sb("w_out", [P, NP, D])
        b_g = sb("b_g", [P, FC])
        b_gh = sb("b_gh", [P, FC])
        b_u = sb("b_u", [P, FC])
        w_d = sb("w_d", [P, FC, D])
        w_up = sb("w_up", [P, EC, D])

        def parts(name, shape):
            return sb(name + "_high", shape, F32R), sb(name + "_low", shape, F32R)

        s_qkv = parts("s_qkv", [P, 3 * DI])
        s_gate = parts("s_gate", [P, H])
        s_g, s_u = parts("s_g", [P, F]), parts("s_u", [P, F])
        s_down = parts("s_down", [P, NE])
        s_sim = parts("s_sim", [P, 2 * RH * NK])

        fwq_sb = sb("fwq_sb", [P, RH, 2, KD])
        fwqT = sb("fwqT", [P, RH * D])
        key_sb = sb("key_sb", [NK, RH, 2 * KD])
        keyT = sb("keyT", [P, RH * NK])
        down_sb = sb("down_sb", [P, EC, D])
        c_sb = sb("c_sb", [B, D])
        c_th = sb("c_th", [B, D])
        c_silu = sb("c_silu", [B, D])
        cT = sb("cT", [P, B])
        wmod_sb = sb("wmod_sb", [P, 6 * D])
        mod_sb = sb("mod_sb", [B, 6 * D])
        mods = sb("mods", [B, NMOD, D])
        sgn = sb("sgn", [B, 2, D])
        mag = sb("mag", [B, 2, D])
        bd_sb = sb("bd_sb", [B, D])
        mods_dram = nc.dram_tensor("mods_dram", [B, NMOD * D], F32, kind="Internal").ap()

        x_in = sb("x_in", [P, TB, D])
        x_res = sb("x_res", [P, TB, D])
        modA = sb("modA", [P, 2, D])
        modB = sb("modB", [P, 3, D])
        modC = sb("modC", [P, 2, D])
        st1 = sb("st1", [P, TB, 6])
        mv1 = sb("mv1", [P, TB, 2])
        ve1 = sb("ve1", [P, TB])
        rs1 = sb("rs1", [P, TB])
        h1 = sb("h1", [P, TB, D])
        sq1 = sb("sq1", [P, TB, D])
        ms1 = sb("ms1", [P, TB])
        me1 = sb("me1", [P, TB])
        rr1 = sb("rr1", [P, TB])
        xr = sb("xr", [P, TB, D])
        xT = parts("xT", [P, N])
        qk = sb("qk", [P, 4, 2 * N])
        v = sb("v", [P, TB, H, DH + 1])
        p_sb = sb("p_sb", [P, 2, 2, SW])
        nmx = sb("nmx", [P, 2, 2, TB])
        pT = sb("pT", [P, 2, 2, SW])
        g_th = sb("g_th", [P, TB, H])
        rden = sb("rden", [P, 2, TB])
        coef = sb("coef", [P, 2, TB])
        ao = sb("ao", [P, 2, TB, P])
        aoT = sb("aoT", [P, NP, N])
        ga_o = sb("ga_o", [P, TB, D])
        x2 = sb("x2", [P, TB, D])
        x2g = sb("x2g", [P, TB, D])
        st2 = sb("st2", [P, TB, 6])
        mv2 = sb("mv2", [P, TB, 2])
        ve2 = sb("ve2", [P, TB])
        rs2 = sb("rs2", [P, TB])
        h2 = sb("h2", [P, TB, D])
        h2T = parts("h2T", [P, N])
        sim = sb("sim", [P, TB, 2, RH, NK])
        tops = sb("tops", [P, 2, TB, RH, TK])
        sxy = sb("sxy", [P, 2, TB, RH, TK])
        xs = sb("xs", [P, TB, RH, NX])
        ys = sb("ys", [P, TB, RH, NK])
        cand = sb("cand", [P, TB, RH, TK, TK])
        top8 = sb("top8", [P, TB, RH, TK])
        e8 = sb("e8", [P, TB, RH, TK])
        zz = sb("zz", [P, TB, RH])
        rz = sb("rz", [P, TB, RH])
        fsum = sb("fsum", [P, TB, RH, NX, NK])
        fexp = sb("fexp", [P, TB, RH, NE])
        chosen = sb("chosen", [P, RH, NE])
        junk = sb("junk", [P, NE])
        wsum = sb("wsum", [P, TB, NE])
        tot = sb("tot", [P, TB])
        u_sb = sb("u_sb", [P, FC, N])
        g_t = sb("g_t", [P, FC, N])
        d_t = sb("d_t", [P, TB, NE])
        eT = sb("eT", [P, TB, EC, P])
        y_g = sb("y_g", [P, TB, D])
        yo = sb("yo", [P, TB, D])

        spare1 = fsum[:, :, :, :, :].rearrange("p k h i j -> p (k h i j)")
        w_qkv, w_gate = spare1[:, 0:3 * DI], spare1[:, 3 * DI:3 * DI + H]
        spare2 = fexp[:, :, :, :].rearrange("p k h e -> p (k h e)")
        w_g, w_u, w_down, w_sim = (spare2[:, n * F:(n + 1) * F] for n in range(4))

        pS = ctx.enter_context(nc.psum_tensor("pS", [P, 2, 2, BANK], F32))
        pW = [ctx.enter_context(nc.psum_tensor(f"pW{n}", [P, BANK], F32)) for n in range(NW)]

        load_cond, load_qkv, load_keys, load_w = sem("load_cond"), sem("load_qkv"), sem("load_keys"), sem("load_w")
        const_pool, const_dve = sem("const_pool"), sem("const_dve")
        su_pe, su_act, su_dve = sem("su_pe"), sem("su_act"), sem("su_dve")
        mods_stored = sem("mods_stored")

        per = {}

        def ev(name, n):
            s = sem(name)
            per[name] = (s, n)
            return name

        def at(name, batch, k):
            return batch * per[name][1] + k

        def S(name):
            return per[name][0]

        x_loaded, res_loaded = ev("x_loaded", 16), ev("res_loaded", 16)
        modA_loaded, modB_loaded, modC_loaded = ev("modA_loaded", 16), ev("modB_loaded", 16), ev("modC_loaded", 16)
        out_stored = ev("out_stored", 16)
        ln1_chain, attn_chain, ffn_chain = ev("ln1_chain", LN1_LINKS), ev("attn_chain", ATTN_LINKS), ev("ffn_chain", FFN_LINKS)
        rstd1_in, rstd1_out = ev("rstd1_in", 2), ev("rstd1_out", 2)
        pool_chain1, pool_chain2 = ev("pool_chain1", 2), ev("pool_chain2", 1)
        xr_ready = ev("xr_ready", 1)
        s_full, s_taken, max_ready = ev("s_full", NP), ev("s_taken", NP), ev("max_ready", NP)
        t_full, pT_ready = ev("t_full", NP), ev("pT_ready", NP)

        xT_high, h2T_high = ev("xT_high", 1), ev("h2T_high", 1)
        x2_ready, x2g_ready = ev("x2_ready", 1), ev("x2g_ready", 1)
        rstd2_in, rstd2_out = ev("rstd2_in", 1), ev("rstd2_out", 1)
        h2_ready = ev("h2_ready", 1)
        top_ready, xs_ready = ev("top_ready", 1), ev("xs_ready", 1)
        masks_ready, fexp_ready = ev("masks_ready", 1), ev("fexp_ready", 2 * TB)
        f_ready, e8_ready = ev("f_ready", TB), ev("e8_ready", 1)
        half_chosen, pool_sum = ev("half_chosen", 1), ev("pool_sum", 7)
        tot_ready = ev("tot_ready", 1)
        gu_act, gu_ready = ev("gu_act", FC), ev("gu_ready", 1)
        d_act = ev("d_act", TB)
        eo_ready = [ev(f"eo{k}_ready", 1) for k in range(TB)]
        yo_ready = ev("yo_ready", 1)

        def jobs_of(step):
            js = []
            if step < 0:
                js += [("QK", 0, "a"), ("QK", 1, "a")]
                js += [("op", k, "f") for k in range(TB)]
                return js + [("V", n, "a") for n in range(TB)]
            early = {1: [("hT", 0)], 2: [("D", 0)], 3: [("D", 1)]}
            js += [(n, k, "f") for n, k in early.get(step, [])]
            if step == NP:
                js.append(("xT", 0, "x"))
            if step in GU_STEPS:
                js.append(("GU", GU_STEPS.index(step), "f"))
            if step == 0:
                js += [("V", n, "a") for n in range(TB, 2 * TB)]
            if step + 2 < NP:
                js.append(("QK", step + 2, "a"))
            if step == 0:
                js.append(("gate", 0, "a"))
            if 2 <= step <= NP:
                js.append(("PV", step - 2, "a"))
            if 3 <= step < NSTEP - 1:
                js.append(("AO", step - 3, "a"))
            if step == NP + 1:
                js.append(("PV", NP - 1, "a"))
            if step == NSTEP - 1:
                js += [("ET", 0, "f"), ("y", 0, "f"), ("ET", 1, "f"), ("AO", NP - 1, "a")]
            if step == 1:
                js += [("sim", k, "f") for k in range(TB)]
            return js

        order = [j for step in range(-1, NSTEP) for j in jobs_of(step)]
        assert len(order) % NW == 0, len(order)
        bank_of, place, count = {}, {}, {}
        for n, (name, k, kind) in enumerate(order):
            key = (n % NW, kind)
            bank_of[name, k] = n % NW
            place[name, k] = count.get(key, 0)
            count[key] = place[name, k] + 1
        work_full = {key: ev(f"work_full_{key[1]}{key[0]}", n) for key, n in count.items()}
        work_free = {key: ev(f"work_free_{key[1]}{key[0]}", n) for key, n in count.items()}
        kind_of = {(name, k): kind for name, k, kind in order}

        class Work:

            def __init__(self, eng, i, attn, ffn):
                self.eng, self.i, self.attn, self.ffn = eng, i, attn, ffn
                self.runs = {"a": attn, "f": ffn, "x": attn and not (isinstance(i, int) and i + 1 >= B)}

            def key(self, name, k):
                return bank_of[name, k], kind_of[name, k]

            def batch(self, name, k):
                return self.i + AHEAD[kind_of[name, k]]

            def bank(self, name, k=0):
                return pW[bank_of[name, k]]

            def before(self, name, k):
                mine = [j for j in order if bank_of[j[0], j[1]] == bank_of[name, k]]
                now = [j for j in mine if self.runs[j[2]]]
                n = [(j[0], j[1]) for j in now].index((name, k))
                if n:
                    return now[n - 1][:2], self.batch(*now[n - 1][:2])
                if not self.ffn:
                    return None
                last = isinstance(self.i, int) and self.i == B
                j = [j for j in mine if not (self.first_loop and j[2] == "f") and not (last and j[2] == "x")][-1]
                return j[:2], self.i - 1 + AHEAD[j[2]]

            first_loop = False

            def wait_free(self, name, k=0):
                prev = self.before(name, k)
                if prev:
                    (pn, pk), batch = prev
                    ev_ = work_free[self.key(pn, pk)]
                    self.eng.wait_ge(S(ev_), at(ev_, batch, place[pn, pk] + 1))

            def filled(self, ins, name, k=0):
                ins.then_inc(S(work_full[self.key(name, k)]), 1)

            def wait_full(self, name, k=0):
                e = work_full[self.key(name, k)]
                self.eng.wait_ge(S(e), at(e, self.batch(name, k), place[name, k] + 1))

            def release(self, ins, name, k=0):
                ins.then_inc(S(work_free[self.key(name, k)]), 1)

        def run(eng, body, tail=1):
            body(0, True, False, False)
            body(1, True, True, True)
            with eng.Fori(2, B - tail) as i:
                body(i, True, True, False)
            for i in range(B - tail, B):
                body(i, True, True, False)
            body(B, False, True, False)

        block = ctx.enter_context(nc.Block())

        @block.sync
        def _(sp):
            sp.dma_start(x_in[:, :, :], x[0:1].rearrange("o (k p) d -> p (o k) d", p=P)).then_inc(S(x_loaded), 16)
            sp.dma_start(w_qkv[:, 0:DI], Wq).then_inc(load_qkv, 16)
            sp.dma_start(w_qkv[:, DI:3 * DI], Wkv).then_inc(load_qkv, 16)
            sp.dma_start(w_gate[:, :], Wgate).then_inc(load_qkv, 16)
            sp.dma_start(nw[:, :], norm_w.rearrange("(d o) -> d o", o=1), allow_slow_non_contiguous=True).then_inc(load_qkv, 16)
            for a in range(2):
                sp.dma_start(fwq_sb[:, :, a, :], fWq[:, a * RH * KD:(a + 1) * RH * KD].rearrange("d (h n) -> d h n", h=RH)).then_inc(load_keys, 16)
            sp.dma_start(key_sb[:, :, :], keys.rearrange("h k p n -> k h (p n)")).then_inc(load_keys, 16)
            sp.dma_start(down_sb[:, :, :], down.rearrange("(c p) d -> p c d", p=P)).then_inc(load_keys, 16)
            sp.dma_start(w_out[:, :, :], Wout.rearrange("(j p) n -> p j n", p=P)).then_inc(load_w, 16)
            sp.dma_start(w_g[:, :], fWg).then_inc(load_w, 16)
            sp.dma_start(w_u[:, :], fWu).then_inc(load_w, 16)
            sp.dma_start(b_g[:, :], fbg.rearrange("(c p) -> p c", p=P), allow_slow_non_contiguous=True).then_inc(load_w, 16)
            sp.dma_start(b_u[:, :], fbu.rearrange("(c p) -> p c", p=P), allow_slow_non_contiguous=True).then_inc(load_w, 16)
            sp.dma_start(w_d[:, :, :], fWd.rearrange("(c p) n -> p c n", p=P)).then_inc(load_w, 16)
            sp.dma_start(w_up[:, :, :], up.rearrange("(c p) n -> p c n", p=P)).then_inc(load_w, 16)

            def load_modA(b):
                sp.dma_start(modA[:, :, :].rearrange("p m d -> p (m d)"),
                             mods_dram[bass.ds(b, 1), SA * D:(CA + 1) * D].broadcast_to([P, 2 * D])).then_inc(S(modA_loaded), 16)

            def load_next(b):
                sp.dma_start(x_in[:, :, :], x[bass.ds(b, 1)].rearrange("o (k p) d -> p (o k) d", p=P)).then_inc(S(x_loaded), 16)
                load_modA(b)

            sp.wait_ge(su_dve, SU_LINKS)
            sp.dma_start(mods_dram, mods[:, :, :].rearrange("b m d -> b (m d)")).then_inc(mods_stored, 16)
            sp.wait_ge(mods_stored, 16)
            load_modA(0)
            sp.wait_ge(S(xr_ready), at(xr_ready, 0, 1))
            load_next(1)

            def body(i, attn, ffn, first):
                if attn:
                    if ffn:
                        sp.wait_ge(S(x2_ready), at(x2_ready, i - 1, 1))
                        sp.wait_ge(S(h2_ready), at(h2_ready, i - 1, 1))
                    sp.dma_start(x_res[:, :, :], x[bass.ds(i, 1)].rearrange("o (k p) d -> p (o k) d", p=P)).then_inc(S(res_loaded), 16)
                    sp.dma_start(modB[:, :, :].rearrange("p m d -> p (m d)"),
                                 mods_dram[bass.ds(i, 1), SB * D:(GA + 1) * D].broadcast_to([P, 3 * D])).then_inc(S(modB_loaded), 16)
                    if not (isinstance(i, int) and i + 2 >= B):
                        sp.wait_ge(S(xr_ready), at(xr_ready, i + 1, 1))
                        load_next(i + 2)
                if ffn:
                    sp.wait_ge(S(yo_ready), at(yo_ready, i - 1, 1))
                    sp.dma_start(out[bass.ds(i - 1, 1)].rearrange("o (k p) d -> p (o k) d", p=P), yo[:, :, :]).then_inc(S(out_stored), 16)
                if attn:
                    sp.dma_start(modC[:, :, :].rearrange("p m d -> p (m d)"),
                                 mods_dram[bass.ds(i, 1), GB * D:(GD + 1) * D].broadcast_to([P, 2 * D])).then_inc(S(modC_loaded), 16)

            run(sp, body, tail=2)
            sp.wait_ge(S(out_stored), at(out_stored, B, 0))

        @block.gpsimd
        def _(pool):
            nc.gpsimd.memset(ident[:, :], 0.0)
            nc.gpsimd.memset(ident_bf[:, :], 0.0)
            nc.gpsimd.memset(mask[:, :], 0.0)
            nc.gpsimd.memset(expo[:, :], -0.5)
            nc.gpsimd.memset(v[:, :, :, DH:DH + 1], 1.0).then_inc(const_pool, 1)
            pool.wait_ge(const_pool, 1)
            nc.gpsimd.affine_select(out=ident[:, :], in_=ident[:, :], compare_op=ALU.not_equal, fill=1.0,
                                    base=0, pattern=[[-1, P]], channel_multiplier=1)
            nc.gpsimd.affine_select(out=ident_bf[:, :], in_=ident_bf[:, :], compare_op=ALU.not_equal, fill=1.0,
                                    base=0, pattern=[[-1, P]], channel_multiplier=1)
            nc.gpsimd.affine_select(out=mask[:, :], in_=mask[:, :], compare_op=ALU.is_ge, fill=MASKED,
                                    base=0, pattern=[[-1, P]], channel_multiplier=1).then_inc(const_pool, 1)

            def apart():
                pool.nop(nofuse=True)

            def rstd1(b):
                pool.wait_ge(S(rstd1_in), at(rstd1_in, b, 1))
                apart()
                nc.gpsimd.tensor_scalar(ve1[:, :], mv1[:, :, 1], LN_EPS, None, ALU.add).then_inc(S(pool_chain1), 1)
                pool.wait_ge(S(pool_chain1), at(pool_chain1, b, 1))
                nc.gpsimd.tensor_tensor(rs1[:, :], ve1[:, :], expo[:, :], ALU.pow).then_inc(S(rstd1_out), 1)
                pool.wait_ge(S(rstd1_in), at(rstd1_in, b, 2))
                apart()
                nc.gpsimd.tensor_scalar(me1[:, :], ms1[:, :], 1.0 / D, RMS_EPS, ALU.mult, ALU.add).then_inc(S(pool_chain1), 1)
                pool.wait_ge(S(pool_chain1), at(pool_chain1, b, 2))
                nc.gpsimd.tensor_tensor(rr1[:, :], me1[:, :], expo[:, :], ALU.pow).then_inc(S(rstd1_out), 1)

            rstd1(0)

            pool.wait_ge(load_w, 112)
            pool.wait_ge(su_act, 5)
            split = ((s_g, w_g), (s_u, w_u), (s_down, w_down), (s_sim, w_sim))
            for (high, low), whole in split:
                ins = nc.gpsimd.tensor_copy(high[:, :], whole[:, :])
            ins.then_inc(const_pool, 1)
            pool.wait_ge(const_pool, 3)
            for (high, low), whole in split:
                ins = nc.gpsimd.tensor_tensor(low[:, :], whole[:, :], high[:, :], ALU.subtract)
            ins.then_inc(const_pool, 1)

            def body(i, attn, ffn, first):
                f = i - 1
                if ffn:
                    pool.wait_ge(S(rstd2_in), at(rstd2_in, f, 1))
                    apart()
                    nc.gpsimd.tensor_scalar(ve2[:, :], mv2[:, :, 1], LN_EPS, None, ALU.add).then_inc(S(pool_chain2), 1)
                    pool.wait_ge(S(pool_chain2), at(pool_chain2, f, 1))
                    nc.gpsimd.tensor_tensor(rs2[:, :], ve2[:, :], expo[:, :], ALU.pow).then_inc(S(rstd2_out), 1)
                    pool.wait_ge(S(x2_ready), at(x2_ready, f, 1))
                    pool.wait_ge(S(modC_loaded), at(modC_loaded, f, 16))
                    nc.gpsimd.tensor_tensor(x2g[:, :, :], x2[:, :, :], modC[:, 1:2, :].broadcast_to([P, TB, D]),
                                            ALU.add).then_inc(S(x2g_ready), 1)
                if attn and not (isinstance(i, int) and i + 1 >= B):
                    rstd1(i + 1)
                if ffn:
                    pool.wait_ge(S(xs_ready), at(xs_ready, f, 1))
                    for k in range(TB):
                        for h in range(RH):
                            ins = nc.gpsimd.tensor_tensor(
                                fsum[:, k, h], xs[:, k, h, :].unsqueeze(2).broadcast_to([P, NX, NK]),
                                ys[:, k, h, :].unsqueeze(1).broadcast_to([P, NX, NK]), ALU.add)
                        ins.then_inc(S(f_ready), 1)
                    pool.wait_ge(S(fexp_ready), at(fexp_ready, f, 2))
                    pool.wait_ge(S(masks_ready), at(masks_ready, f, 1))
                    nc.gpsimd.tensor_tensor(fexp[:, 0], fexp[:, 0], chosen[:, :, :], ALU.mult).then_inc(S(pool_sum), 1)
                    pool.wait_ge(S(pool_sum), at(pool_sum, f, 1))
                    nc.gpsimd.tensor_tensor(fexp[:, 0, 0:2, :], fexp[:, 0, 0:2, :], fexp[:, 0, 2:4, :], ALU.add).then_inc(S(pool_sum), 1)
                    pool.wait_ge(S(pool_sum), at(pool_sum, f, 2))
                    nc.gpsimd.tensor_tensor(wsum[:, 0, :], fexp[:, 0, 0, :], fexp[:, 0, 1, :], ALU.add).then_inc(S(pool_sum), 1)
                    pool.wait_ge(S(half_chosen), at(half_chosen, f, 1))
                    nc.gpsimd.tensor_tensor(fexp[:, 1, 0:2, :], fexp[:, 1, 0:2, :], rz[:, 1, 0:2].unsqueeze(2).broadcast_to([P, 2, NE]),
                                            ALU.mult).then_inc(S(pool_sum), 1)
                    pool.wait_ge(S(pool_sum), at(pool_sum, f, 4))
                    nc.gpsimd.tensor_tensor(wsum[:, 1, :], fexp[:, 1, 0, :], fexp[:, 1, 1, :], ALU.add).then_inc(S(pool_sum), 1)
                    pool.wait_ge(S(tot_ready), at(tot_ready, f, 1))
                    apart()
                    nc.gpsimd.tensor_scalar(tot[:, 0:1], tot[:, 0:1], -1.0, float(RH), ALU.mult, ALU.add).then_inc(S(pool_sum), 1)
                    pool.wait_ge(S(pool_sum), at(pool_sum, f, 6))
                    nc.gpsimd.tensor_tensor(wsum[:, 0, NE - 1:NE], wsum[:, 0, NE - 1:NE], tot[:, 0:1], ALU.add).then_inc(S(pool_sum), 1)
                    pool.wait_ge(S(pool_sum), at(pool_sum, f, 7))
                    e = work_free[bank_of["D", 0], "f"]
                    pool.wait_ge(S(e), at(e, f, place["D", 0] + 1))
                    nc.gpsimd.tensor_tensor(d_t[:, 0, :], d_t[:, 0, :], wsum[:, 0, :], ALU.mult).then_inc(S(eo_ready[0]), 1)

            run(pool, body)

        @block.scalar
        def _(act):
            act.dma_start(c_sb[:, :], cond).then_inc(load_cond, 16)
            act.dma_start(wmod_sb[:, :], wmod).then_inc(load_cond, 16)
            act.dma_start(bd_sb[:, :], fbd.rearrange("(o d) -> o d", o=1).broadcast_to([B, D])).then_inc(load_cond, 16)
            act.wait_ge(load_cond, 48)
            nc.scalar.activation(c_th[:, :], c_sb[:, :], ACT.Tanh, scale=0.5).then_inc(su_act, 1)

            def expert_exp(b, k, half):
                if half == 0:
                    act.wait_ge(S(f_ready), at(f_ready, b, k + 1))
                hs = slice(half * RH // 2, (half + 1) * RH // 2)
                ins = nc.scalar.activation(fexp[:, k, hs].rearrange("p h e -> p (h e)"),
                                           fsum[:, k, hs].rearrange("p h i j -> p (h i j)"), ACT.Exp)
                ins.then_inc(S(fexp_ready), 1)

            def body(i, attn, ffn, first):
                w = Work(act, i, attn, ffn)
                w.first_loop = first
                f = i - 1

                def evacuate(dst, src, name, k=0):
                    w.wait_full(name, k)
                    w.release(nc.scalar.copy(dst, src), name, k)

                def exp_scores(p):
                    act.wait_ge(S(max_ready), at(max_ready, i, p + 1))
                    for h in range(2):
                        nc.scalar.activation(p_sb[:, p % 2, h, 0:P], pS[:, p % 2, h, 0:P], ACT.Exp, bias=nmx[:, p % 2, h, 0:1])
                        ins = nc.scalar.activation(p_sb[:, p % 2, h, P:SW], pS[:, p % 2, h, P:SW], ACT.Exp, bias=nmx[:, p % 2, h, 1:2])
                    ins.then_inc(S(s_taken), 1)

                def copy_transposes(p):
                    act.wait_ge(S(t_full), at(t_full, i, p + 1))
                    if p >= 2:
                        w.wait_full("PV", p - 2)
                    nc.scalar.copy(pT[:, p % 2], pS[:, p % 2, :, 0:SW]).then_inc(S(pT_ready), 1)

                if attn:
                    for p in range(2):
                        evacuate(qk[:, p, :], w.bank("QK", p)[:, :], "QK", p)

                def values(n):
                    k, half = divmod(n, 2)
                    evacuate(v[:, k, half * 8:half * 8 + 8, 0:DH],
                             w.bank("V", n)[:, :].rearrange("p (h d) -> p h d", h=8), "V", n)

                if attn:
                    for n in range(TB):
                        values(n)
                for s in range(NSTEP):
                    if w.runs["x"] and s == NP:
                        w.wait_full("xT")
                        nc.scalar.copy(xT[0][:, :], w.bank("xT")[:, 0:N]).then_inc(S(xT_high), 1)
                    if ffn and s == 1:
                        w.wait_full("hT")
                        nc.scalar.copy(h2T[0][:, :], w.bank("hT")[:, 0:N]).then_inc(S(h2T_high), 1)
                    early_copy = ffn and s in (4, 5)
                    if attn and early_copy:
                        copy_transposes(s - 1)
                    if ffn:
                        if s == 4:
                            act.wait_ge(S(top_ready), at(top_ready, f, 1))
                            nc.scalar.activation(e8[:, :, :, :], top8[:, :, :, :], ACT.Exp).then_inc(S(e8_ready), 1)
                        if s in (2, 3):
                            k = s - 2
                            w.wait_full("D", k)
                            nc.scalar.activation(d_t[:, k, :], w.bank("D", k)[:, :], ACT.Tanh, scale=0.5).then_inc(S(d_act), 1)
                        if s in GU_STEPS:
                            c = GU_STEPS.index(s)
                            w.wait_full("GU", c)
                            bank = w.bank("GU", c)
                            nc.scalar.activation(g_t[:, c, :], bank[:, 0:N], ACT.Tanh, bias=b_gh[:, c:c + 1], scale=0.5)
                            nc.scalar.activation(u_sb[:, c, :], bank[:, N:2 * N], ACT.Identity,
                                                 bias=b_u[:, c:c + 1]).then_inc(S(gu_act), 1)
                    if attn and s == NP:
                        evacuate(aoT[:, s - 3, :], w.bank("AO", s - 3)[:, 0:N], "AO", s - 3)
                    if ffn and s == NP:
                        act.wait_ge(S(pool_sum), at(pool_sum, f, 3))
                        nc.scalar.activation(junk[:, :], wsum[:, 0, :], ACT.Copy, accum_out=tot[:, 0:1]).then_inc(S(tot_ready), 1)
                    if attn and 1 <= s < NP + 1 and not early_copy:
                        copy_transposes(s - 1)
                    if attn and s < NP:
                        exp_scores(s)
                    if ffn and s == NSTEP - 1:
                        evacuate(eT[:, 1].rearrange("p c t -> p (c t)"), w.bank("ET", 1)[:, :], "ET", 1)
                    if ffn and s in (4, 5, 6):
                        expert_exp(f, int(s > 4), int(s > 5))
                    if attn and s == 0:
                        for n in range(TB, 2 * TB):
                            values(n)
                    if attn and s + 2 < NP:
                        if s + 2 >= 4:
                            act.wait_ge(S(s_full), at(s_full, i, s - 1))
                        evacuate(qk[:, (s + 2) % 4, :], w.bank("QK", s + 2)[:, :], "QK", s + 2)
                    if attn and s == 0:
                        w.wait_full("gate")
                        w.release(nc.scalar.activation(g_th[:, :, :].rearrange("p k h -> p (k h)"), w.bank("gate")[:, 0:TB * H],
                                                       ACT.Tanh, scale=0.5), "gate")
                    if attn and 3 <= s and s != NP:
                        evacuate(aoT[:, s - 3, :], w.bank("AO", s - 3)[:, 0:N], "AO", s - 3)
                    if ffn and s == NP + 1:
                        evacuate(eT[:, 0].rearrange("p c t -> p (c t)"), w.bank("ET", 0)[:, :], "ET", 0)
                    if ffn and s == 1:
                        for k in range(TB):
                            evacuate(sim[:, k].rearrange("p a h n -> p (a h n)"), w.bank("sim", k)[:, :], "sim", k)
                    if ffn:
                        if s == 4:
                            expert_exp(f, 0, 1)

            act.wait_ge(su_pe, 3)
            nc.scalar.copy(fwqT[:, :], pS[:, 0, 0, :]).then_inc(su_act, 1)
            act.wait_ge(su_pe, 4)
            nc.scalar.copy(keyT[:, :], pS[:, 0, 1, 0:RH * NK]).then_inc(su_act, 1)
            act.wait_ge(su_pe, 5)
            nc.scalar.copy(w_down[:, :], pW[2][:, :]).then_inc(su_act, 1)
            act.wait_ge(su_pe, 6)
            nc.scalar.copy(w_sim[:, 0:RH * NK], pS[:, 1, 0, 0:RH * NK])
            nc.scalar.copy(w_sim[:, RH * NK:2 * RH * NK], pS[:, 1, 1, 0:RH * NK]).then_inc(su_act, 1)
            w = Work(act, -1, True, False)
            w.wait_full("xT")
            nc.scalar.copy(xT[0][:, :], w.bank("xT")[:, 0:N]).then_inc(S(xT_high), 1)
            run(act, body)

        @block.vector
        def _(dve):
            n_links = {ln1_chain: 0, attn_chain: 0, ffn_chain: 0}

            def link(ins, chain, b):
                n_links[chain] += 1
                ins.then_inc(S(chain), 1)
                dve.wait_ge(S(chain), at(chain, b, n_links[chain]))

            def apart():
                dve.nop(nofuse=True)

            def done(chain):
                assert n_links[chain] == per[chain][1], (chain, n_links[chain])
                n_links[chain] = 0

            su = [0]

            def su_link(ins):
                su[0] += 1
                ins.then_inc(su_dve, 1)
                dve.wait_ge(su_dve, su[0])

            def ln1_stats(b):
                dve.wait_ge(S(x_loaded), at(x_loaded, b, 16))
                for k in range(TB):
                    ins = nc.vector.bn_stats(st1[:, k, :], x_in[:, k, :])
                link(ins, ln1_chain, b)
                apart()
                for k in range(TB):
                    ins = nc.vector.bn_aggr(mv1[:, k, :], st1[:, k, :])
                ins.then_inc(S(rstd1_in), 1)

            def ln1_modulate(b):
                dve.wait_ge(S(rstd1_out), at(rstd1_out, b, 1))
                dve.wait_ge(S(modA_loaded), at(modA_loaded, b, 16))
                for k in range(TB):
                    ins = nc.vector.tensor_scalar(h1[:, k, :], x_in[:, k, :], mv1[:, k, 0:1], rs1[:, k:k + 1], ALU.subtract, ALU.mult)
                link(ins, ln1_chain, b)
                link(nc.vector.tensor_tensor(h1[:, :, :], h1[:, :, :], modA[:, 1:2, :].broadcast_to([P, TB, D]), ALU.mult), ln1_chain, b)
                link(nc.vector.tensor_tensor(h1[:, :, :], h1[:, :, :], modA[:, 0:1, :].broadcast_to([P, TB, D]), ALU.add), ln1_chain, b)
                for k in range(TB):
                    ins = nc.vector.tensor_tensor_reduce(out=sq1[:, k, :], in0=h1[:, k, :], in1=h1[:, k, :], scale=1.0, scalar=0.0,
                                                         op0=ALU.mult, op1=ALU.add, accum_out=ms1[:, k:k + 1])
                ins.then_inc(S(rstd1_in), 1)

            def ln1_rms(b):
                dve.wait_ge(S(rstd1_out), at(rstd1_out, b, 2))
                for k in range(TB):
                    ins = nc.vector.tensor_scalar(xr[:, k, :], h1[:, k, :], rr1[:, k:k + 1], None, ALU.mult)
                ins.then_inc(S(xr_ready), 1)
                done(ln1_chain)

            def low_part(w, high, parts, name, b):
                dve.wait_ge(S(high), at(high, b, 1))
                w.release(nc.vector.tensor_tensor(parts[1][:, :], w.bank(name)[:, 0:N], parts[0][:, :], ALU.subtract), name)

            dve.wait_ge(load_cond, 48)
            dve.wait_ge(su_act, 1)
            su_link(nc.vector.scalar_tensor_tensor(out=c_silu[:, :], in0=c_th[:, :], scalar=1.0, in1=c_sb[:, :], op0=ALU.add, op1=ALU.mult))
            su_link(nc.vector.tensor_scalar(c_silu[:, :], c_silu[:, :], 0.5, None, ALU.mult))
            dve.wait_ge(su_pe, 1)
            su_link(nc.vector.tensor_copy(cT[:, :], pW[0][:, 0:B]))
            dve.wait_ge(su_pe, 2)
            nc.vector.tensor_copy(mod_sb[:, 0:BANK], pW[0][0:B, :])
            su_link(nc.vector.tensor_copy(mod_sb[:, BANK:6 * D], pW[1][0:B, 0:6 * D - BANK]))
            m6 = mod_sb[:, :].rearrange("b (m d) -> b m d", m=6)
            gates = m6[:, 2:6:3, :]
            nc.vector.tensor_copy(mods[:, SA, :], m6[:, 0, :])
            nc.vector.tensor_scalar(mods[:, CA, :], m6[:, 1, :], 1.0, None, ALU.add)
            nc.vector.tensor_copy(mods[:, SB, :], m6[:, 3, :])
            nc.vector.tensor_scalar(mods[:, CB, :], m6[:, 4, :], 1.0, None, ALU.add)
            nc.vector.tensor_scalar(sgn[:, :, :], gates, 0.0, 2.0, ALU.is_ge, ALU.mult)
            su_link(nc.vector.scalar_tensor_tensor(out=mag[:, :, :], in0=gates, scalar=-1.0, in1=gates, op0=ALU.mult, op1=ALU.max))
            su_link(nc.vector.tensor_scalar(sgn[:, :, :], sgn[:, :, :], -1.0, None, ALU.add))
            su_link(nc.vector.scalar_tensor_tensor(out=mods[:, GA:GB + 1, :], in0=mag[:, :, :], scalar=0.25, in1=sgn[:, :, :],
                                                   op0=ALU.max, op1=ALU.mult))
            su_link(nc.vector.tensor_tensor(mods[:, GD, :], mods[:, GB, :], bd_sb[:, :], ALU.mult))
            ln1_stats(0)
            dve.wait_ge(load_qkv, 64)
            nc.vector.tensor_scalar(w_qkv[:, 0:DI], w_qkv[:, 0:DI], nw[:, 0:1], SCALE, ALU.mult, ALU.mult)
            nc.vector.tensor_scalar(w_qkv[:, DI:3 * DI], w_qkv[:, DI:3 * DI], nw[:, 0:1], None, ALU.mult)
            nc.vector.tensor_scalar(w_gate[:, :], w_gate[:, :], nw[:, 0:1], None, ALU.mult).then_inc(const_dve, 1)
            dve.wait_ge(const_dve, 1)
            nc.vector.tensor_copy(s_gate[0][:, :], w_gate[:, :])
            nc.vector.tensor_copy(s_qkv[0][:, :], w_qkv[:, :]).then_inc(const_dve, 1)
            dve.wait_ge(const_dve, 2)
            ln1_modulate(0)
            ln1_rms(0)
            nc.vector.tensor_tensor(s_gate[1][:, :], w_gate[:, :], s_gate[0][:, :], ALU.subtract)
            nc.vector.tensor_tensor(s_qkv[1][:, :], w_qkv[:, :], s_qkv[0][:, :], ALU.subtract).then_inc(const_dve, 1)
            low_part(Work(dve, -1, True, False), xT_high, xT, "xT", 0)
            dve.wait_ge(load_w, 112)
            nc.vector.tensor_scalar(w_out[:, :, :], w_out[:, :, :], 0.5, None, ALU.mult)
            nc.vector.tensor_scalar(w_d[:, :, :], w_d[:, :, :], 0.5, None, ALU.mult)
            nc.vector.tensor_scalar(w_up[:, :, :], w_up[:, :, :], 0.5, None, ALU.mult)
            nc.vector.tensor_scalar(b_gh[:, :], b_g[:, :], 0.5, None, ALU.mult).then_inc(const_dve, 1)

            def body(i, attn, ffn, first):
                w = Work(dve, i, attn, ffn)
                w.first_loop = first
                f = i - 1
                ahead = attn and not (isinstance(i, int) and i + 1 >= B)

                def choose(h):
                    dve.wait_ge(S(fexp_ready), at(fexp_ready, f, TB + 1 + h // 2))
                    ins = nc.vector.scalar_tensor_tensor(
                        out=fexp[:, 1, h, :], in0=fsum[:, 1, h].rearrange("p i j -> p (i j)"), scalar=top8[:, 1, h, TK - 1:TK],
                        in1=fexp[:, 1, h, :], op0=ALU.is_ge, op1=ALU.mult)
                    if h == 1:
                        ins.then_inc(S(half_chosen), 1)
                    if h == RH - 1:
                        link(ins, ffn_chain, f)

                def bias_product(c):
                    dve.wait_ge(S(gu_act), at(gu_act, f, c + 1))
                    w.release(nc.vector.scalar_tensor_tensor(out=u_sb[:, c, :], in0=w.bank("GU", c)[:, 0:N], scalar=b_g[:, c:c + 1],
                                                             in1=u_sb[:, c, :], op0=ALU.add, op1=ALU.mult), "GU", c)

                def gate_product(c):
                    e = work_free[w.key("GU", c)]
                    dve.wait_ge(S(e), at(e, f, place["GU", c] + 1))
                    ins = nc.vector.scalar_tensor_tensor(out=g_t[:, c, :], in0=g_t[:, c, :], scalar=1.0, in1=u_sb[:, c, :],
                                                         op0=ALU.add, op1=ALU.mult)
                    if c == FC - 1:
                        ins.then_inc(S(gu_ready), 1)

                if ffn:
                    dve.wait_ge(S(res_loaded), at(res_loaded, f, 16))
                    dve.wait_ge(S(modB_loaded), at(modB_loaded, f, 16))
                    for k in range(TB):
                        w.wait_full("op", k)
                        ins = nc.vector.tensor_tensor(ga_o[:, k, :], w.bank("op", k)[:, 0:D], modB[:, 2, :], ALU.mult)
                        w.release(ins, "op", k)
                    e = work_free[w.key("op", TB - 1)]
                    dve.wait_ge(S(e), at(e, f, place["op", TB - 1] + 1))
                    ins = nc.vector.tensor_tensor(x2[:, :, :], ga_o[:, :, :], x_res[:, :, :], ALU.add)
                    ins.then_inc(S(x2_ready), 1)
                    dve.wait_ge(S(x2_ready), at(x2_ready, f, 1))
                    for k in range(TB):
                        ins = nc.vector.bn_stats(st2[:, k, :], x2[:, k, :])
                    link(ins, ffn_chain, f)
                    apart()
                    for k in range(TB):
                        ins = nc.vector.bn_aggr(mv2[:, k, :], st2[:, k, :])
                    ins.then_inc(S(rstd2_in), 1)
                for s in range(NSTEP):
                    if ffn and s == 1:
                        low_part(w, h2T_high, h2T, "hT", f)
                    if attn and s < NP:
                        dve.wait_ge(S(s_full), at(s_full, i, s + 1))
                        nc.vector.reduce_max(nmx[:, s % 2, :, 0], pS[:, s % 2, :, 0:P], AX_X, negate=True)
                        nc.vector.reduce_max(nmx[:, s % 2, :, 1], pS[:, s % 2, :, P:SW], AX_X, negate=True).then_inc(S(max_ready), 1)
                    if ffn:
                        if s == 6:
                            choose(0)
                            choose(1)
                        if s == 7:
                            choose(2)
                        if s in (2, 3):
                            k = s - 2
                            dve.wait_ge(S(d_act), at(d_act, f, k + 1))
                            ins = nc.vector.scalar_tensor_tensor(out=d_t[:, k, :], in0=d_t[:, k, :], scalar=1.0, in1=w.bank("D", k)[:, :],
                                                                 op0=ALU.add, op1=ALU.mult)
                            w.release(ins, "D", k)
                    if ffn and s == GU_STEPS[-1]:
                        bias_product(FC - 1)
                        gate_product(FC - 1)
                    if attn and 2 <= s < NP + 2:
                        p = s - 2
                        if p == 0:
                            e = work_free[w.key("gate", 0)]
                            dve.wait_ge(S(e), at(e, i, place["gate", 0] + 1))
                        w.wait_full("PV", p)
                        pv = w.bank("PV", p)[:, 0:2 * TB * (DH + 1)].rearrange("p (h k e) -> p h k e", h=2, k=TB)
                        link(nc.vector.reciprocal(rden[:, :, :], pv[:, :, :, DH]), attn_chain, i)
                        link(nc.vector.scalar_tensor_tensor(out=coef[:, :, :], in0=g_th[:, :, 2 * p:2 * p + 2].rearrange("p k h -> p h k"),
                                                            scalar=1.0, in1=rden[:, :, :], op0=ALU.add, op1=ALU.mult), attn_chain, i)
                        if p >= 2:
                            e = work_full[w.key("AO", p - 2)]
                            dve.wait_ge(S(e), at(e, i, place["AO", p - 2] + 1))
                        ins = nc.vector.tensor_tensor(ao[:, p % 2].rearrange("p k (h d) -> p h k d", h=2), pv[:, :, :, 0:DH],
                                                      coef[:, :, :].unsqueeze(3).broadcast_to([P, 2, TB, DH]), ALU.mult)
                        w.release(ins, "PV", p)
                    if w.runs["x"] and s == NP:
                        low_part(w, xT_high, xT, "xT", i + 1)
                    if ffn:
                        if s == 0:
                            dve.wait_ge(S(rstd2_out), at(rstd2_out, f, 1))
                            for k in range(TB):
                                ins = nc.vector.tensor_scalar(h2[:, k, :], x2[:, k, :], mv2[:, k, 0:1], rs2[:, k:k + 1], ALU.subtract, ALU.mult)
                            link(ins, ffn_chain, f)
                            link(nc.vector.tensor_tensor(h2[:, :, :], h2[:, :, :], modB[:, 1:2, :].broadcast_to([P, TB, D]), ALU.mult), ffn_chain, f)
                            nc.vector.tensor_tensor(h2[:, :, :], h2[:, :, :], modB[:, 0:1, :].broadcast_to([P, TB, D]), ALU.add).then_inc(S(h2_ready), 1)
                        if s in GU_STEPS[:-1]:
                            bias_product(GU_STEPS.index(s))
                        if s == 2:
                            for k in range(TB):
                                e = work_free[w.key("sim", k)]
                                dve.wait_ge(S(e), at(e, f, place["sim", k] + 1))
                                apart()
                                for a in range(2):
                                    for h in range(RH):
                                        ins = nc.vector.max(tops[:, a, k, h, :], sim[:, k, a, h, :])
                            link(ins, ffn_chain, f)
                            nc.vector.tensor_tensor(xs[:, :, :, :], sim[:, :, 0, :, 0:NX], tops[:, 0, :, :, 0:1].broadcast_to([P, TB, RH, NX]),
                                                    ALU.subtract)
                            nc.vector.tensor_tensor(ys[:, :, :, :], sim[:, :, 1, :, :], tops[:, 1, :, :, 0:1].broadcast_to([P, TB, RH, NK]),
                                                    ALU.subtract).then_inc(S(xs_ready), 1)
                        if s == 3:
                            link(nc.vector.tensor_tensor(sxy[:, :, :, :, :].rearrange("p a k h t -> p (a k h) t"),
                                                         tops[:, :, :, :, :].rearrange("p a k h t -> p (a k h) t"),
                                                         tops[:, :, :, :, 0:1].rearrange("p a k h t -> p (a k h) t").broadcast_to([P, 2 * TB * RH, TK]),
                                                         ALU.subtract), ffn_chain, f)
                            link(nc.vector.tensor_tensor(
                                cand[:, :, :, :, :].rearrange("p k h a b -> p (k h) a b"),
                                sxy[:, 0].rearrange("p k h a -> p (k h) a").unsqueeze(3).broadcast_to([P, TB * RH, TK, TK]),
                                sxy[:, 1].rearrange("p k h a -> p (k h) a").unsqueeze(2).broadcast_to([P, TB * RH, TK, TK]),
                                ALU.add), ffn_chain, f)
                            apart()
                            for kk in range(TB):
                                for h in range(RH):
                                    ins = nc.vector.max(top8[:, kk, h, :], cand[:, kk, h].rearrange("p a b -> p (a b)"))
                            ins.then_inc(S(top_ready), 1)
                        if s == 4:
                            dve.wait_ge(S(e8_ready), at(e8_ready, f, 1))
                            link(nc.vector.reduce_sum(zz[:, :, :], e8[:, :, :, :], AX_X), ffn_chain, f)
                            link(nc.vector.reciprocal(rz[:, :, :], zz[:, :, :]), ffn_chain, f)
                            dve.wait_ge(S(f_ready), at(f_ready, f, 1))
                            for h in range(RH):
                                ins = nc.vector.tensor_scalar(chosen[:, h, :], fsum[:, 0, h].rearrange("p i j -> p (i j)"),
                                                              top8[:, 0, h, TK - 1:TK], rz[:, 0, h:h + 1], ALU.is_ge, ALU.mult)
                            ins.then_inc(S(masks_ready), 1)
                        if s == 7:
                            choose(3)
                        if s in MLP_STEPS[:-1]:
                            gate_product(MLP_STEPS.index(s))
                        if s == 8:
                            dve.wait_ge(S(pool_sum), at(pool_sum, f, 5))
                            for h in range(2, RH):
                                link(nc.vector.scalar_tensor_tensor(out=wsum[:, 1, :], in0=fexp[:, 1, h, :], scalar=rz[:, 1, h:h + 1],
                                                                    in1=wsum[:, 1, :], op0=ALU.mult, op1=ALU.add,
                                                                    accum_out=tot[:, 1:2] if h == RH - 1 else None), ffn_chain, f)
                            link(nc.vector.tensor_scalar(tot[:, 1:2], tot[:, 1:2], -1.0, float(RH), ALU.mult, ALU.add), ffn_chain, f)
                            link(nc.vector.tensor_tensor(wsum[:, 1, NE - 1:NE], wsum[:, 1, NE - 1:NE], tot[:, 1:2], ALU.add), ffn_chain, f)
                            e = work_free[w.key("D", 1)]
                            dve.wait_ge(S(e), at(e, f, place["D", 1] + 1))
                            nc.vector.tensor_tensor(d_t[:, 1, :], d_t[:, 1, :], wsum[:, 1, :], ALU.mult).then_inc(S(eo_ready[1]), 1)
                    if ahead:
                        if s == 0:
                            ln1_stats(i + 1)
                        if s == 1:
                            ln1_modulate(i + 1)
                        if s == 5:
                            ln1_rms(i + 1)
                if ffn:
                    w.wait_full("y")
                    dve.wait_ge(S(modC_loaded), at(modC_loaded, f, 16))
                    ins = nc.vector.tensor_tensor(y_g[:, :, :], w.bank("y")[:, 0:N].rearrange("p (k d) -> p k d", k=TB),
                                                  modC[:, 0:1, :].broadcast_to([P, TB, D]), ALU.mult)
                    w.release(ins, "y")
                    e = work_free[w.key("y", 0)]
                    dve.wait_ge(S(e), at(e, f, place["y", 0] + 1))
                    dve.wait_ge(S(x2g_ready), at(x2g_ready, f, 1))
                    if not first:
                        dve.wait_ge(S(out_stored), at(out_stored, f, 0))
                    nc.vector.tensor_tensor(yo[:, :, :], y_g[:, :, :], x2g[:, :, :], ALU.add).then_inc(S(yo_ready), 1)
                    done(ffn_chain)
                if attn:
                    done(attn_chain)

            run(dve, body)

        @block.tensor
        def _(pe):
            mm, tp = nc.tensor.matmul, nc.tensor.transpose
            pe.wait_ge(const_pool, 2)
            pe.wait_ge(su_dve, 2)
            tp(pW[0][:, 0:B], c_silu[:, :], ident[0:B, 0:B]).then_inc(su_pe, 1)
            pe.wait_ge(su_dve, 3)
            pe.wait_ge(load_cond, 48)
            mm(pW[0][0:B, :], cT[:, :], wmod_sb[:, 0:BANK], start=True, stop=True)
            mm(pW[1][0:B, 0:6 * D - BANK], cT[:, :], wmod_sb[:, BANK:6 * D], start=True, stop=True).then_inc(su_pe, 1)
            pe.wait_ge(load_keys, 64)
            for h in range(RH):
                ins = tp(pS[:, 0, 0, h * D:(h + 1) * D], fwq_sb[:, h].rearrange("d p n -> d (p n)"), ident[:, :])
            ins.then_inc(su_pe, 1)
            for h in range(RH):
                ins = tp(pS[:, 0, 1, h * NK:(h + 1) * NK], key_sb[:, h, :], ident[0:NK, 0:NK])
            ins.then_inc(su_pe, 1)
            for c in range(EC):
                ins = tp(pW[2][:, c * P:(c + 1) * P], down_sb[:, c, :], ident[:, :])
            ins.then_inc(su_pe, 1)
            pe.wait_ge(su_act, 3)
            for a in range(2):
                rows = slice(a * KD, (a + 1) * KD)
                for h in range(RH):
                    ins = mm(pS[:, 1, a, h * NK:(h + 1) * NK], fwqT[rows, h * D:(h + 1) * D], keyT[rows, h * NK:(h + 1) * NK],
                             start=True, stop=True)
            ins.then_inc(su_pe, 1)
            pe.wait_ge(su_act, 5)
            pe.wait_ge(su_dve, 4)

            def transpose_rows(w, name, rows):
                for k in range(TB):
                    ins = tp(w.bank(name)[:, k * P:(k + 1) * P], rows[:, k, :], ident[:, :])
                w.filled(ins, name)

            def mm3(o, lhs, rhs):
                mm(o, lhs[0], rhs[0], start=True, stop=False)
                mm(o, lhs[0], rhs[1], start=False, stop=False)
                return mm(o, lhs[1], rhs[0], start=False, stop=True)

            def cols(parts, lo, hi):
                return parts[0][:, lo:hi], parts[1][:, lo:hi]

            def body(i, attn, ffn, first):
                w = Work(pe, i, attn, ffn)
                w.first_loop = first
                f = i - 1

                def released(name, k=0):
                    e = work_free[w.key(name, k)]
                    pe.wait_ge(S(e), at(e, w.batch(name, k), place[name, k] + 1))

                def project_qk(p):
                    w.wait_free("QK", p)
                    bank = w.bank("QK", p)
                    mm3(bank[:, 0:N], cols(s_qkv, p * P, (p + 1) * P), cols(xT, 0, N))
                    w.filled(mm3(bank[:, N:2 * N], cols(s_qkv, DI + p * P, DI + (p + 1) * P), cols(xT, 0, N)), "QK", p)

                def project_v(n):
                    k, half = divmod(n, 2)
                    w.wait_free("V", n)
                    w.filled(mm3(w.bank("V", n)[:, :], cols(xT, k * P, (k + 1) * P),
                                 cols(s_qkv, 2 * DI + half * BANK, 2 * DI + (half + 1) * BANK)), "V", n)

                def scores(p):
                    released("QK", p)
                    if p >= 2 or not (isinstance(i, int) and i == 0):
                        pe.wait_ge(S(pT_ready), at(pT_ready, i, p - 1))
                    ps = pS[:, p % 2]
                    for h in range(2):
                        r = slice(h * DH, (h + 1) * DH)
                        mm(ps[:, h, 0:P], qk[r, p % 4, 0:P], qk[r, p % 4, N:N + P], start=True, stop=False, skip_group_check=True)
                    for h in range(2):
                        r = slice(h * DH, (h + 1) * DH)
                        mm(ps[:, h, P:SW], qk[r, p % 4, P:N], qk[r, p % 4, N:2 * N], start=False, stop=False, skip_group_check=True)
                    for h in range(2):
                        mm(ps[:, h, 0:P], ident_bf[:, :], mask[:, :], start=False, stop=True, skip_group_check=True)
                        ins = mm(ps[:, h, 2 * P:SW], ident_bf[:, :], mask[:, :], start=False, stop=True, skip_group_check=True)
                    ins.then_inc(S(s_full), 1)

                def transpose_scores(p):
                    pe.wait_ge(S(s_taken), at(s_taken, i, p + 1))
                    for h in range(2):
                        for b in range(BLOCKS):
                            ins = tp(pS[:, p % 2, h, b * P:(b + 1) * P], p_sb[:, p % 2, h, b * P:(b + 1) * P], ident[:, :])
                    ins.then_inc(S(t_full), 1)

                def weigh_values(p):
                    if p == 0:
                        released("V", 2 * TB - 1)
                    pe.wait_ge(S(pT_ready), at(pT_ready, i, p + 1))
                    w.wait_free("PV", p)
                    bank = w.bank("PV", p)
                    E1 = DH + 1
                    for h in range(2):
                        hh = 2 * p + h
                        o0, o1 = (2 * h) * E1, (2 * h + 1) * E1
                        mm(bank[:, o0:o0 + E1], pT[:, p % 2, h, 0:P], v[:, 0, hh, :], start=True, stop=True)
                        mm(bank[:, o1:o1 + E1], pT[:, p % 2, h, P:2 * P], v[:, 0, hh, :], start=True, stop=False)
                        ins = mm(bank[:, o1:o1 + E1], pT[:, p % 2, h, 2 * P:3 * P], v[:, 1, hh, :], start=False, stop=True)
                    w.filled(ins, "PV", p)

                def project_gate():
                    w.wait_free("gate")
                    for k in range(TB):
                        ins = mm3(w.bank("gate")[:, k * H:(k + 1) * H], cols(xT, k * P, (k + 1) * P), cols(s_gate, 0, H))
                    w.filled(ins, "gate")

                def transpose_out(p):
                    released("PV", p)
                    w.wait_free("AO", p)
                    for k in range(TB):
                        ins = tp(w.bank("AO", p)[:, k * P:(k + 1) * P], ao[:, p % 2, k, :], ident[:, :])
                    w.filled(ins, "AO", p)

                def transpose_x():
                    if w.runs["x"]:
                        pe.wait_ge(S(xr_ready), at(xr_ready, i + 1, 1))
                        w.wait_free("xT")
                        transpose_rows(w, "xT", xr)

                def second_half(step):
                    if step == 1:
                        if first:
                            pe.wait_ge(const_pool, 4)
                        pe.wait_ge(S(h2_ready), at(h2_ready, f, 1))
                        w.wait_free("hT")
                        transpose_rows(w, "hT", h2)
                    if step in (2, 3):
                        k = step - 2
                        w.wait_free("D", k)
                        w.filled(mm3(w.bank("D", k)[:, :], cols(h2T, k * P, (k + 1) * P), cols(s_down, 0, NE)), "D", k)
                    if step in GU_STEPS:
                        c = GU_STEPS.index(step)
                        w.wait_free("GU", c)
                        bank = w.bank("GU", c)
                        mm3(bank[:, 0:N], cols(s_g, c * P, (c + 1) * P), cols(h2T, 0, N))
                        w.filled(mm3(bank[:, N:2 * N], cols(s_u, c * P, (c + 1) * P), cols(h2T, 0, N)), "GU", c)
                    if step == NSTEP - 1:
                        transpose_experts(1)
                        project_experts(0)

                def transpose_experts(n):
                    pe.wait_ge(S(eo_ready[n]), at(eo_ready[n], f, 1))
                    w.wait_free("ET", n)
                    for c in range(EC):
                        ins = tp(w.bank("ET", n)[:, c * P:(c + 1) * P], d_t[:, n, c * P:(c + 1) * P], ident[:, :])
                    w.filled(ins, "ET", n)

                def project_mlp(k):
                    for c in range(FC):
                        mm(w.bank("y")[:, k * D:(k + 1) * D], g_t[:, c, k * P:(k + 1) * P], w_d[:, c, :],
                           start=k == 0 and c == 0, stop=False, skip_group_check=True)

                def project_experts(k):
                    released("ET", k)
                    for c in range(EC):
                        ins = mm(w.bank("y")[:, k * D:(k + 1) * D], eT[:, k, c, :], w_up[:, c, :],
                                 start=False, stop=c == EC - 1, skip_group_check=True)
                    if k == TB - 1:
                        w.filled(ins, "y")

                if attn:
                    e = work_free[w.key("xT", 0)]
                    pe.wait_ge(S(e), at(e, i, 1))
                    project_qk(0)
                    project_qk(1)
                if first:
                    pe.wait_ge(const_dve, 4)
                if ffn:
                    e = work_free[bank_of["AO", NP - 1], "a"]
                    pe.wait_ge(S(e), at(e, f, place["AO", NP - 1] + 1))
                    for k in range(TB):
                        w.wait_free("op", k)
                        for p in range(NP):
                            ins = mm(w.bank("op", k)[:, 0:D], aoT[:, p, k * P:(k + 1) * P], w_out[:, p, :],
                                     start=p == 0, stop=p == NP - 1)
                        w.filled(ins, "op", k)
                if attn:
                    for n in range(TB):
                        project_v(n)
                for s in range(NSTEP):
                    if attn and s < NP:
                        scores(s)
                    if s == NP:
                        transpose_x()
                    if ffn:
                        second_half(s)
                    if attn and 1 <= s < NP:
                        transpose_scores(s - 1)
                    if attn and s == 0:
                        for n in range(TB, 2 * TB):
                            project_v(n)
                    if attn and s + 2 < NP:
                        project_qk(s + 2)
                    if attn and s == 0:
                        project_gate()
                    if attn and 2 <= s <= NP:
                        weigh_values(s - 2)
                    if attn and 3 <= s and s != NP + 1:
                        transpose_out(s - 3)
                    if attn and s == NP:
                        transpose_scores(NP - 1)
                    if ffn and s == NP + 1:
                        pe.wait_ge(S(gu_ready), at(gu_ready, f, 1))
                        w.wait_free("y")
                        project_mlp(0)
                    if attn and s == NP + 1:
                        transpose_out(s - 3)
                        weigh_values(NP - 1)
                    if ffn and s == NP + 1:
                        transpose_experts(0)
                        project_mlp(1)
                    if ffn and s == NSTEP - 1:
                        project_experts(1)
                    if ffn and s == 1:
                        released("hT")
                        for k in range(TB):
                            w.wait_free("sim", k)
                            w.filled(mm3(w.bank("sim", k)[:, :], cols(h2T, k * P, (k + 1) * P), cols(s_sim, 0, 2 * RH * NK)), "sim", k)

            pe.wait_ge(S(xr_ready), at(xr_ready, 0, 1))
            transpose_rows(Work(pe, -1, True, False), "xT", xr)
            pe.wait_ge(const_dve, 3)
            run(pe, body)


LN1_LINKS, ATTN_LINKS, FFN_LINKS, SU_LINKS = 4, 16, 13, 8

_INS = ['L0_attn_tokens', 'L0_attn_norm_w', 'L0_attn_Wq', 'L0_attn_Wkv', 'L0_attn_Wout', 'L0_attn_Wg', 'L0_ffn_Wg',
        'L0_ffn_bg', 'L0_ffn_Wu', 'L0_ffn_bu', 'L0_ffn_Wd', 'L0_ffn_bd', 'L0_ffn_Wq', 'L0_ffn_keys', 'L0_ffn_down_embed',
        'L0_ffn_up_embed', 'L0_c', 'L0_wmod']


def kernel(**inputs):
    import numpy as _np
    import concourse.bacc as _bacc
    from concourse import mybir as _mybir
    from concourse.bass_utils import run_bass_kernel_spmd as _run

    nc = _bacc.Bacc("TRN2", target_bir_lowering=False, num_devices=1)
    arrays, args = {}, []
    for name in _INS:
        a = _np.ascontiguousarray(inputs[name])
        arrays[f"in_{name}"] = a
        args.append(nc.dram_tensor(f"in_{name}", a.shape, _mybir.dt.from_np(a.dtype), kind="ExternalInput").ap())
    out = nc.dram_tensor("out", (B, N, D), _mybir.dt.float32, kind="ExternalOutput").ap()
    program(nc, *args, out)
    r = _run(nc, [arrays], core_ids=[0])
    return r.results[0]["out"]
```
